# Optimizing a Trainium2 kernel written in Bass

```python
import numpy as np
import jax
import jax.numpy as jnp

def _softmax(x, axis=-1):
    return jax.nn.softmax(x, axis=axis)

def _gelu(x):
    return jax.nn.gelu(x, approximate=True)

def _silu(x):
    return jax.nn.silu(x)

def _sigmoid(x):
    return jax.nn.sigmoid(x)

def _layernorm(x, axis=-1, eps=1e-05):
    m = jnp.mean(x, axis=axis, keepdims=True)
    v = jnp.var(x, axis=axis, keepdims=True)
    return (x - m) / jnp.sqrt(v + eps)

def _scatter_add(tgt, idx, src, axis=0):
    return tgt.at[idx].add(src)

def _segment_sum(src, seg, n):
    return jax.ops.segment_sum(src, seg, n)
kernel_name = 'mk_xattn_ffn_d1_seqx_r8_6cf414'

def setup_inputs(seed: int=0):
    np.random.seed(seed)
    _w = jnp.asarray

    def _rec_inputs():
        import jax
        import jax.numpy as jnp
        _rk = jax.random.key(seed)
        x = 7.22e-05 + 1 * jax.random.normal(jax.random.fold_in(_rk, 1), (2, 512, 128), jnp.float32)
        _lenS = 512 - jax.random.randint(jax.random.fold_in(_rk, 7), (2,), 0, max(1, 512 // 4) + 1, jnp.int32)
        _lenS2 = 77 - jax.random.randint(jax.random.fold_in(_rk, 8), (2,), 0, max(1, 77 // 4) + 1, jnp.int32)
        _ctx_1024P = jax.random.normal(jax.random.fold_in(_rk, 11), (2, 16, 128), jnp.float32)
        _ctx_1024c = jax.random.dirichlet(jax.random.fold_in(_rk, 511), 0.3 * jnp.ones((16,), jnp.float32), (2, 77))
        _ctx_1024t = jnp.einsum('bsk,bkd->bsd', _ctx_1024c, _ctx_1024P)
        _ctx_1024t = _ctx_1024t * jax.lax.rsqrt(jnp.mean(jnp.square(_ctx_1024t)) + 1e-12) * 0.953939
        ctx_1024 = 4.13588e-05 + 0.999923 * (_ctx_1024t + 0.3 * jax.random.normal(jax.random.fold_in(_rk, 611), (2, 77, 128), jnp.float32))
        return (x, ctx_1024)
    x, ctx_1024 = _rec_inputs()

    def _L0_xattn_setup():
        import jax, jax.numpy as jnp
        import numpy as np
        D = 128
        B, SQ, SKV = (4, 256, 256)
        key = jax.random.key(seed)
        ks = jax.random.split(key, 8)
        s = 1.0 / np.sqrt(D)
        return {'x': jax.random.normal(ks[0], (B, SQ, D), jnp.float32), 'context': jax.random.normal(ks[1], (B, SKV, D), jnp.float32), 'Wq': jax.random.uniform(ks[2], (D, D), jnp.float32, -s, s), 'bq': jnp.zeros((D,), jnp.float32), 'Wk': jax.random.uniform(ks[3], (D, D), jnp.float32, -s, s), 'bk': jnp.zeros((D,), jnp.float32), 'Wv': jax.random.uniform(ks[4], (D, D), jnp.float32, -s, s), 'bv': jnp.zeros((D,), jnp.float32)}
    _L0_xattn_all = _L0_xattn_setup()
    _L0_xattn_in = {k: v for k, v in _L0_xattn_all.items() if k in ('Wq', 'bq', 'Wk', 'bk', 'Wv', 'bv')}
    del _L0_xattn_all

    def _L0_ffn_setup():
        import jax, jax.numpy as jnp
        import numpy as np
        B, S, D, E, K = (4, 256, 128, 8, 2)
        H = 4 * D
        key = jax.random.key(seed)
        ks = jax.random.split(key, 4)
        sc = lambda n: 1.0 / np.sqrt(n)
        return {'x': jax.random.normal(ks[0], (B, S, D), jnp.float32), 'gate_w': jax.random.normal(ks[1], (D, E), jnp.float32) * sc(D), 'gate_b': jnp.zeros((E,), jnp.float32), 'w1': jax.random.normal(ks[2], (E, D, H), jnp.float32) * sc(D), 'b1': jnp.zeros((E, H), jnp.float32), 'w2': jax.random.normal(ks[3], (E, H, D), jnp.float32) * sc(H), 'b2': jnp.zeros((E, D), jnp.float32)}
    _L0_ffn_all = _L0_ffn_setup()
    _L0_ffn_in = {k: v for k, v in _L0_ffn_all.items() if k in ('gate_w', 'gate_b', 'w1', 'b1', 'w2', 'b2')}
    del _L0_ffn_all
    return {'x': x, 'ctx_1024': ctx_1024, 'L0_xattn_Wq': _L0_xattn_in['Wq'], 'L0_xattn_bq': _L0_xattn_in['bq'], 'L0_xattn_Wk': _L0_xattn_in['Wk'], 'L0_xattn_bk': _L0_xattn_in['bk'], 'L0_xattn_Wv': _L0_xattn_in['Wv'], 'L0_xattn_bv': _L0_xattn_in['bv'], 'L0_ffn_gate_w': _L0_ffn_in['gate_w'], 'L0_ffn_gate_b': _L0_ffn_in['gate_b'], 'L0_ffn_w1': _L0_ffn_in['w1'], 'L0_ffn_b1': _L0_ffn_in['b1'], 'L0_ffn_w2': _L0_ffn_in['w2'], 'L0_ffn_b2': _L0_ffn_in['b2']}

def reference(x, ctx_1024, L0_xattn_Wq, L0_xattn_bq, L0_xattn_Wk, L0_xattn_bk, L0_xattn_Wv, L0_xattn_bv, L0_ffn_gate_w, L0_ffn_gate_b, L0_ffn_w1, L0_ffn_b1, L0_ffn_w2, L0_ffn_b2):
    import jax
    import jax.numpy as jnp

    def _L0_xattn_ref(x, context, Wq, bq, Wk, bk, Wv, bv):
        import jax, jax.numpy as jnp
        import numpy as np
        D = 128
        B, SQ, SKV = (4, 256, 256)
        Q = x @ Wq + bq
        K = context @ Wk + bk
        V = context @ Wv + bv
        scale = 1.0 / np.sqrt(D).astype(np.float32)
        scores = jnp.einsum('bqd,bkd->bqk', Q, K) * scale
        attn = jax.nn.softmax(scores, axis=-1)
        out = jnp.einsum('bqk,bkd->bqd', attn, V)
        return out

    def _L0_ffn_ref(x, gate_w, gate_b, w1, b1, w2, b2):
        import jax, jax.numpy as jnp
        import numpy as np
        B, S, D, E, K = (4, 256, 128, 8, 2)
        H = 4 * D
        Bx, Sx, Dx = x.shape
        n_exp = w1.shape[0]
        logits = jnp.einsum('bsd,de->bse', x, gate_w) + gate_b
        scores = jax.nn.softmax(logits, axis=-1)
        topk_s, topk_i = jax.lax.top_k(scores, K)
        onehot = jax.nn.one_hot(topk_i, n_exp, dtype=scores.dtype)
        dispatch = jnp.einsum('bske,bsk->bse', onehot, topk_s)
        xf = x.reshape(-1, Dx)
        wf = dispatch.reshape(-1, n_exp)
        out = jnp.zeros_like(xf)
        for i in range(n_exp):
            wi = wf[:, i:i + 1]
            h = jax.nn.relu(xf * wi @ w1[i] + b1[i])
            y = h @ w2[i] + b2[i]
            out = jnp.where(wi > 0, y, out)
        return out.reshape(Bx, Sx, Dx)
    x = x + _L0_xattn_ref(_layernorm(x, axis=-1), ctx_1024, L0_xattn_Wq, L0_xattn_bq, L0_xattn_Wk, L0_xattn_bk, L0_xattn_Wv, L0_xattn_bv)
    x = x + _L0_ffn_ref(_layernorm(x, axis=-1), L0_ffn_gate_w, L0_ffn_gate_b, L0_ffn_w1, L0_ffn_b1, L0_ffn_w2, L0_ffn_b2)
    return x

_drawn_inputs = setup_inputs


def setup_inputs(seed=0):
    import zlib

    import numpy as np

    out = dict(_drawn_inputs(seed))
    spreads = {'L0_xattn_bq': (0.0, 0.312),
     'L0_xattn_bk': (0.0, 0.8),
     'L0_xattn_bv': (0.0, 0.1),
     'L0_ffn_gate_b': (0.0, 0.1),
     'L0_ffn_b1': (0.0, 0.1),
     'L0_ffn_b2': (0.0, 0.1)}
    factors = {}
    for name, (base, spread) in spreads.items():
        noise = np.random.default_rng([zlib.crc32(name.encode()), seed]).standard_normal(out[name].shape)
        drawn = base * np.exp(spread * noise) if base else spread * noise
        out[name] = jnp.asarray(drawn.astype(out[name].dtype))
    for name, factor in factors.items():
        out[name] = (out[name] * factor).astype(out[name].dtype)
    return out
```

```python
from contextlib import ExitStack

import concourse.bass as bass
from concourse import mybir

F32 = mybir.dt.float32
BF16 = mybir.dt.bfloat16
F16 = mybir.dt.float16
U32 = mybir.dt.uint32
I32 = mybir.dt.int32
ALU = mybir.AluOpType
ACT = mybir.ActivationFunctionType
AX_X = mybir.AxisListType.X

P = 128
EPS = 1e-5
BIG = 4096.0


def xattn_moe_kernel(nc, x, ctx_in, Wq, bq, Wk, bk, Wv, bv, gate_w, gate_b, w1, b1, w2, b2, out):
    B, SQ, D = x.shape
    SKV = ctx_in.shape[1]
    E, _, H = w1.shape
    N = B * SQ
    I = SQ // P
    T = B * I
    J = T + E - 1
    C = H // P
    SCALE = 1.0 / float(D) ** 0.5
    ROW = D + 4
    RING = 3
    assert D == P and J % RING == 0 and SKV <= P and B == 2

    rows_dram = nc.dram_tensor("token_rows", [N, ROW], F32).ap()
    bias_dram = nc.dram_tensor("bias_parts", [3, E * (H + D)], BF16).ap()

    with ExitStack() as ctx:
        def sb(name, shape, dt=F32):
            return ctx.enter_context(nc.sbuf_tensor(name, shape, dt))

        def sem(name):
            return ctx.enter_context(nc.semaphore(name))

        bank = [ctx.enter_context(nc.psum_tensor(f"bank{i}", [P, 512], F32)) for i in range(8)]

        x_sb = sb("x_sb", [P, B, I, D])
        ctx_sb = sb("ctx_sb", [SKV, B, D])
        wq_sb, wk_sb, wv_sb = sb("wq_sb", [P, D]), sb("wk_sb", [P, D]), sb("wv_sb", [P, D])
        bq_sb, bk_sb, bv_sb = sb("bq_sb", [P, 1]), sb("bk_sb", [P, 1]), sb("bv_sb", [1, D])
        gw_sb, gb_sb = sb("gw_sb", [P, E]), sb("gb_sb", [P, E])
        w1_sb = sb("w1_sb", [P, E, H])
        w2_sb = sb("w2_sb", [P, E, C, D])
        b12_sb = sb("b12_sb", [P, E * (H + D) // P])
        ident = sb("ident", [P, P])
        before = sb("before", [P, P], BF16)
        ones_bf = sb("ones_bf", [P, P], BF16)
        ones_row = sb("ones_row", [1, P])
        half = sb("half", [P, I])
        lo_iota = sb("lo_iota", [P, P], F16)
        rev = sb("rev", [P, E])
        thr = sb("thr", [P, J + 1])
        jot = sb("jot", [1, J])
        token = sb("token", [P, B, I])
        ones_e = sb("ones_e", [P, E])
        ctxT, wqT = sb("ctxT", [P, B, SKV]), sb("wqT", [P, P])
        bq_wide = sb("bq_wide", [P, P])
        kT, score_w, score_b = sb("kT", [P, B, SKV]), sb("score_w", [P, B, SKV]), sb("score_b", [P, B, SKV])
        v_sb = sb("v_sb", [SKV, B, D])
        stats, mv, rstd = sb("stats", [P, T, 6]), sb("mv", [P, T, 2]), sb("rstd", [P, T])
        varp = sb("varp", [P, T])
        xn, xnT = sb("xn", [P, B, I, D]), sb("xnT", [P, B, I, P])
        s_sb, p_sb = sb("s_sb", [P, B, I, SKV]), sb("p_sb", [P, B, I, SKV])
        smax, ssum, sinv = sb("smax", [P, B, I]), sb("ssum", [P, B, I]), sb("sinv", [P, B, I])
        pT = sb("pT", [SKV, B, I, P])
        rows = sb("rows", [P, B, I, ROW])
        stats2, mv2, rstd2, varp2 = sb("stats2", [P, T, 6]), sb("mv2", [P, T, 2]), sb("rstd2", [P, T]), sb("varp2", [P, T])
        xn2, xn2T = sb("xn2", [P, B, I, D]), sb("xn2T", [P, B, I, P])
        lg, sc, t3 = sb("lg", [P, T, E]), sb("sc", [P, T, E]), sb("t3", [P, T, E])
        m0, m1, m2, k1, k2 = (sb(n, [P, T]) for n in ("m0", "m1", "m2", "k1", "k2"))
        gsum, gw = sb("gsum", [P, T]), sb("gwt", [P, T])
        chosen = sb("chosen", [P, T + 1, E], BF16)
        ntile, upto, first = sb("ntile", [P, E]), sb("upto", [P, E]), sb("first", [P, E])
        cmp8, cmpj = sb("cmp8", [P, E, T]), sb("cmpj", [1, J, E])
        expert_f, expert_of = sb("expert_f", [1, J]), sb("expert_of", [1, J], I32)
        pos, lo, nge = sb("pos", [P, T]), sb("lo", [P, T]), sb("nge", [P, T])
        ge = sb("ge", [P, T, J + 1])
        hit = sb("hit", [P, T, 2, J], F16)
        lo_hot = sb("lo_hot", [P, T, P], F16)
        src_row, dst_row = sb("src_row", [P, J], U32), sb("dst_row", [P, J], U32)
        emptyv = sb("emptyv", [P, J])
        part = sb("part", [P, 3, E * (H + D) // P], BF16)
        rest = sb("rest", [P, 2, E * (H + D) // P])
        bias_sb = sb("bias_sb", [3, E * (H + D)], BF16)
        gat = sb("gat", [P, J, ROW])
        xs, xsT = sb("xs", [P, D]), sb("xsT", [P, P])
        h_sb, hT = sb("h_sb", [P, C, P]), sb("hT", [P, C, P])
        y_sb = sb("y_sb", [P, J, D])

        x_loaded = [sem(f"x_loaded{b}") for b in range(B)]
        ctx_loaded, wq_loaded, wk_loaded, wv_loaded = sem("ctx_loaded"), sem("wq_loaded"), sem("wk_loaded"), sem("wv_loaded")
        bqk_loaded, gate_loaded, experts_loaded = sem("bqk_loaded"), sem("gate_loaded"), sem("experts_loaded")
        b12_loaded, bias_stored, bias_ready = sem("b12_loaded"), sem("bias_stored"), sem("bias_ready")
        pool_chain, dve_chain = sem("pool_chain"), sem("dve_chain")
        consts_ready, wide_ready = sem("consts_ready"), sem("wide_ready")
        prep_ps, prep_sb = sem("prep_ps"), sem("prep_sb")
        var_ready, rstd_ready = sem("var_ready"), sem("rstd_ready")
        xn_ready, xnT_ps, xnT_ready = sem("xn_ready"), sem("xnT_ps"), sem("xnT_ready")
        s_ps, s_ready, p_ready, pT_ps, pT_ready, o_ps = (sem(n) for n in (
            "s_ps", "s_ready", "p_ready", "pT_ps", "pT_ready", "o_ps"))
        logits_ps, logits_ready, exp_ready = sem("logits_ps"), sem("logits_ready"), sem("exp_ready")
        chosen_ready, rank_ps, hot_ready, slot_ps = (sem(n) for n in ("chosen_ready", "rank_ps", "hot_ready", "slot_ps"))
        parts_ready, rows_ready, rows_stored = sem("parts_ready"), sem("rows_ready"), sem("rows_stored")
        slots_ready, expert_ready = sem("slots_ready"), sem("expert_ready")
        gathered = [sem(f"gathered{k}") for k in range(RING)]
        xs_ready, xsT_ps, xsT_ready, h_ps, h_ready, hT_ps, hT_ready, y_ps, y_ready, y_stored = (sem(n) for n in (
            "xs_ready", "xsT_ps", "xsT_ready", "h_ps", "h_ready", "hT_ps", "hT_ready", "y_ps", "y_ready", "y_stored"))

        x_dram = x.rearrange("b (p i) d -> b p i d", i=I)
        rows_store = rows_dram.rearrange("(b p i) c -> b p i c", b=B, i=I)
        out_dram = out.rearrange("b s d -> (b s) d")
        nb1, nb2 = E * H // P, E * D // P
        block = ctx.enter_context(nc.Block())

        @block.sync
        def _(sp):
            for b in range(B):
                sp.dma_start(x_sb[:, b], x_dram[b]).then_inc(x_loaded[b], 16)
            sp.dma_start(wq_sb[:, :], Wq).then_inc(wq_loaded, 16)
            sp.dma_start(bq_sb[:, :], bq.rearrange("(d a) -> d a", a=1)).then_inc(bqk_loaded, 16)
            sp.dma_start(b12_sb[:, 0:nb1], b1.rearrange("e h -> (e h)").rearrange("(p f) -> p f", p=P)).then_inc(b12_loaded, 16)
            sp.dma_start(b12_sb[:, nb1:], b2.rearrange("e h -> (e h)").rearrange("(p f) -> p f", p=P)).then_inc(b12_loaded, 16)
            half_e = E // 2
            for e in (0, half_e):
                sp.dma_start(w1_sb[:, e:e + half_e, :], w1[e:e + half_e].rearrange("e d h -> d e h")).then_inc(experts_loaded, 16)
                sp.dma_start(w2_sb[:, e:e + half_e, :, :],
                             w2[e:e + half_e].rearrange("e (p c) d -> p e c d", c=C)).then_inc(experts_loaded, 16)
            sp.wait_ge(parts_ready, 1)
            sp.dma_start(bias_dram[:, 0:E * H].rearrange("j (p f) -> p j f", p=P), part[:, :, 0:nb1]).then_inc(bias_stored, 16)
            sp.dma_start(bias_dram[:, E * H:].rearrange("j (p f) -> p j f", p=P), part[:, :, nb1:]).then_inc(bias_stored, 16)
            sp.wait_ge(bias_stored, 32)
            sp.dma_start(bias_sb[:, :], bias_dram).then_inc(bias_ready, 16)
            sp.wait_ge(rows_ready, 1)
            for b in range(B):
                sp.dma_start(rows_store[b], rows[:, b]).then_inc(rows_stored, 16)
            sp.wait_ge(y_stored, 16 * J)

        @block.gpsimd
        def _(pool):
            made = [0]

            def step(ins):
                made[0] += 1
                ins.then_inc(pool_chain, 1)

            step(pool.memset(ident[:, :], 0.0))
            step(pool.memset(before[:, :], 1.0))
            step(pool.memset(half[:, :], -0.5))
            pool.wait_ge(pool_chain, made[0])
            pool.affine_select(out=ident[:, :], in_=ident[:, :], compare_op=ALU.not_equal, fill=1.0, base=0,
                               pattern=[[-1, P]], channel_multiplier=1).then_inc(consts_ready, 1)
            step(pool.affine_select(out=before[:, :], in_=before[:, :], compare_op=ALU.is_gt, fill=0.0, base=0,
                                    pattern=[[1, P]], channel_multiplier=-1))
            step(pool.memset(ones_bf[:, :], 1.0))
            step(pool.memset(ones_row[:, :], 1.0))
            step(pool.memset(ones_e[:, :], 1.0))
            step(pool.memset(chosen[:, T, :], 0.0))
            step(pool.memset(rows[:, :, :, D + 2:ROW], 0.0))
            step(pool.iota(lo_iota[:, :], pattern=[[1, P]], base=-P, channel_multiplier=0,
                           allow_small_or_imprecise_dtypes=True))
            step(pool.iota(rev[:, :], pattern=[[-1, E]], base=E, channel_multiplier=0, allow_small_or_imprecise_dtypes=True))
            step(pool.iota(thr[:, :], pattern=[[P, J + 1]], base=0, channel_multiplier=0, allow_small_or_imprecise_dtypes=True))
            step(pool.iota(jot[:, :], pattern=[[1, J]], base=0, channel_multiplier=0, allow_small_or_imprecise_dtypes=True))
            pool.iota(token[:, :, :], pattern=[[SQ, B], [1, I]], base=0, channel_multiplier=I,
                      allow_small_or_imprecise_dtypes=True).then_inc(consts_ready, 1)
            for g in range(2 * B):
                src, dst = (varp, rstd) if g < B else (varp2, rstd2)
                t = slice((g % B) * I, (g % B + 1) * I)
                pool.wait_ge(var_ready, g + 1)
                pool.tensor_tensor(dst[:, t], src[:, t], half[:, :], ALU.pow).then_inc(rstd_ready, 1)
            pool.wait_ge(rows_stored, 16 * B)
            pool.wait_ge(slots_ready, 1)

            def gather(j):
                pool.indirect_dma_start(gat[:, j, :], None, rows_dram,
                                        bass.IndirectOffsetOnAxis(src_row[:, j:j + 1], 0)).then_inc(gathered[j % RING], 16)

            def scatter(j):
                pool.wait_ge(y_ready, j + 1)
                pool.indirect_dma_start(out_dram, bass.IndirectOffsetOnAxis(dst_row[:, j:j + 1], 0), y_sb[:, j, :], None,
                                        bounds_check=N - 1, oob_is_err=False).then_inc(y_stored, 16)

            for j in range(RING):
                gather(j)
            for j in range(J):
                if j + RING < J:
                    pool.wait_ge(xs_ready, j + 1)
                    gather(j + RING)
                scatter(j)

        @block.scalar
        def _(act):
            act.dma_start(ctx_sb[:, :, :], ctx_in.rearrange("b s d -> s b d")).then_inc(ctx_loaded, 16)
            act.dma_start(wk_sb[:, :], Wk).then_inc(wk_loaded, 16)
            act.dma_start(bk_sb[:, :], bk.rearrange("(d a) -> d a", a=1)).then_inc(bqk_loaded, 16)
            act.dma_start(wv_sb[:, :], Wv).then_inc(wv_loaded, 16)
            act.dma_start(bv_sb[:, :], bv.rearrange("(a d) -> a d", a=1)).then_inc(wv_loaded, 16)
            act.dma_start(gw_sb[:, :], gate_w).then_inc(gate_loaded, 16)
            act.dma_start(gb_sb[:, :], gate_b.rearrange("(a e) -> a e", a=1).to_broadcast([P, E])).then_inc(gate_loaded, 16)
            act.wait_ge(prep_ps, 1)
            act.copy(ctxT[:, :, :], bank[0][:, 0:B * SKV].rearrange("p (b s) -> p b s", b=B)).then_inc(prep_sb, 1)
            act.wait_ge(prep_ps, 2)
            act.copy(wqT[:, :], bank[1][:, 0:P]).then_inc(prep_sb, 1)
            act.wait_ge(prep_ps, 3)
            act.wait_ge(bqk_loaded, 32)
            act.activation(kT[:, :, :], bank[2][:, 0:B * SKV].rearrange("p (b s) -> p b s", b=B), ACT.Identity,
                           bias=bk_sb[:, 0:1]).then_inc(prep_sb, 1)
            act.wait_ge(prep_ps, 4)
            act.copy(score_w[:, :, :], bank[3][:, 0:B * SKV].rearrange("p (b s) -> p b s", b=B)).then_inc(prep_sb, 1)
            act.wait_ge(prep_ps, 5)
            act.copy(score_b[:, :, :], bank[4][:, 0:B * SKV].rearrange("p (b s) -> p b s", b=B)).then_inc(prep_sb, 1)
            act.wait_ge(prep_ps, 6)
            act.copy(v_sb[:, :, :], bank[5][0:SKV, 0:B * D].rearrange("p (b d) -> p b d", b=B)).then_inc(prep_sb, 1)
            for b in range(B):
                act.wait_ge(xnT_ps, b + 1)
                act.copy(xnT[:, b], bank[6 + b][:, :].rearrange("p (i q) -> p i q", i=I)).then_inc(xnT_ready, 1)
            for b in range(B):
                act.wait_ge(s_ready, b + 1)
                for i in range(I):
                    act.activation(p_sb[:, b, i], s_sb[:, b, i], ACT.Exp, bias=smax[:, b, i:i + 1], scale=SCALE,
                                   accum_out=ssum[:, b, i:i + 1]).then_inc(p_ready, 1)
            for b in range(B):
                act.wait_ge(pT_ps, b + 1)
                act.copy(pT[:, b], bank[2 + b][0:SKV, :].rearrange("p (i q) -> p i q", i=I)).then_inc(pT_ready, 1)
            for b in range(B):
                act.wait_ge(xnT_ps, B + b + 1)
                act.copy(xn2T[:, b], bank[6 + b][:, :].rearrange("p (i q) -> p i q", i=I)).then_inc(xnT_ready, 1)
            act.wait_ge(logits_ready, 1)
            act.activation(sc[:, :, :], lg[:, :, :], ACT.Exp).then_inc(exp_ready, 1)
            with act.Fori(0, J) as j:
                act.wait_ge(h_ps, j + 1)
                act.activation(h_sb[:, :, :], bank[4][:, :].rearrange("p (q c) -> p c q", c=C), ACT.Relu).then_inc(h_ready, 1)

        @block.vector
        def _(dve):
            made = [0]

            def step(ins):
                made[0] += 1
                ins.then_inc(dve_chain, 1)

            def settled():
                dve.wait_ge(dve_chain, made[0])

            def over_e(a, n=E):
                return a.unsqueeze(2).to_broadcast([a.shape[0], a.shape[1], n])

            def over_t(a, n=T):
                return a.unsqueeze(1).to_broadcast([a.shape[0], n, a.shape[1]])

            def variance(src, b, stats, mv, varp):
                for i in range(I):
                    step(dve.bn_stats(stats[:, b * I + i, :], src(i)))
                settled()
                for i in range(I):
                    step(dve.bn_aggr(mv[:, b * I + i, :], stats[:, b * I + i, :]))
                settled()
                t = slice(b * I, (b + 1) * I)
                dve.tensor_scalar(varp[:, t], mv[:, t, 1], EPS, None, ALU.add).then_inc(var_ready, 1)

            def normalise(src, dst, b, mv, rstd):
                for i in range(I):
                    t = b * I + i
                    ins = dve.tensor_scalar(dst[:, b, i], src(i), mv[:, t, 0:1], rstd[:, t:t + 1], ALU.subtract, ALU.mult)
                ins.then_inc(xn_ready, 1)

            for b in range(B):
                dve.wait_ge(x_loaded[b], 16)
                variance(lambda i: x_sb[:, b, i], b, stats, mv, varp)
            for b in range(B):
                dve.wait_ge(rstd_ready, b + 1)
                normalise(lambda i: x_sb[:, b, i], xn, b, mv, rstd)
            dve.wait_ge(bqk_loaded, 32)
            dve.tensor_copy(bq_wide[:, :], bq_sb[:, 0:1].to_broadcast([P, P])).then_inc(wide_ready, 1)
            dve.wait_ge(b12_loaded, 32)
            step(dve.tensor_copy(part[:, 0], b12_sb[:, :]))
            settled()
            step(dve.tensor_tensor(rest[:, 0], b12_sb[:, :], part[:, 0], ALU.subtract))
            settled()
            step(dve.tensor_copy(part[:, 1], rest[:, 0]))
            settled()
            step(dve.tensor_tensor(rest[:, 1], rest[:, 0], part[:, 1], ALU.subtract))
            settled()
            dve.tensor_copy(part[:, 2], rest[:, 1]).then_inc(parts_ready, 1)
            dve.wait_ge(prep_sb, 5)
            for b in range(B):
                dve.wait_ge(s_ps, b + 1)
                step(dve.tensor_tensor(s_sb[:, b], bank[b][:, 0:I * SKV].rearrange("p (i s) -> p i s", i=I),
                                       over_t(score_b[:, b], I), ALU.add))
                settled()
                step(dve.tensor_reduce(sinv[:, b], s_sb[:, b], AX_X, ALU.max))
                settled()
                dve.tensor_scalar(smax[:, b], sinv[:, b], -SCALE, None, ALU.mult).then_inc(s_ready, 1)
            for b in range(B):
                dve.wait_ge(p_ready, I * (b + 1))
                step(dve.reciprocal(sinv[:, b], ssum[:, b]))
                settled()
                dve.wait_ge(o_ps, b + 1)
                for i in range(I):
                    step(dve.scalar_tensor_tensor(out=rows[:, b, i, 0:D], in0=bank[4 + b][:, i * D:(i + 1) * D],
                                                  scalar=sinv[:, b, i:i + 1], in1=x_sb[:, b, i], op0=ALU.mult, op1=ALU.add))
                settled()
                variance(lambda i: rows[:, b, i, 0:D], b, stats2, mv2, varp2)
            for b in range(B):
                dve.wait_ge(rstd_ready, B + b + 1)
                normalise(lambda i: rows[:, b, i, 0:D], xn2, b, mv2, rstd2)
            dve.wait_ge(gate_loaded, 32)
            dve.wait_ge(consts_ready, 2)
            dve.wait_ge(logits_ps, 1)
            step(dve.tensor_tensor(t3[:, :, :], bank[0][:, 0:T * E].rearrange("p (t e) -> p t e", t=T), over_t(gb_sb[:, :]), ALU.add))
            settled()
            step(dve.tensor_reduce(m0[:, :], t3[:, :, :], AX_X, ALU.max))
            settled()
            dve.tensor_tensor(lg[:, :, :], t3[:, :, :], over_e(m0[:, :]), ALU.subtract).then_inc(logits_ready, 1)
            dve.wait_ge(exp_ready, 1)
            step(dve.tensor_reduce(gsum[:, :], sc[:, :, :], AX_X, ALU.add))
            settled()
            step(dve.reciprocal(gsum[:, :], gsum[:, :]))
            settled()
            step(dve.tensor_tensor(lg[:, :, :], sc[:, :, :], over_e(gsum[:, :]), ALU.mult))
            settled()
            step(dve.tensor_reduce(m1[:, :], lg[:, :, :], AX_X, ALU.max))
            settled()
            step(dve.tensor_tensor(t3[:, :, :], lg[:, :, :], over_e(m1[:, :]), ALU.is_equal))
            settled()
            step(dve.tensor_tensor(t3[:, :, :], t3[:, :, :], over_t(rev[:, :]), ALU.mult))
            settled()
            step(dve.tensor_reduce(k1[:, :], t3[:, :, :], AX_X, ALU.max))
            settled()
            step(dve.tensor_tensor(t3[:, :, :], over_t(rev[:, :]), over_e(k1[:, :]), ALU.is_equal))
            settled()
            step(dve.scalar_tensor_tensor(out=sc[:, :, :], in0=t3[:, :, :], scalar=-2.0, in1=lg[:, :, :], op0=ALU.mult, op1=ALU.add))
            settled()
            step(dve.tensor_reduce(m2[:, :], sc[:, :, :], AX_X, ALU.max))
            settled()
            step(dve.tensor_tensor(t3[:, :, :], sc[:, :, :], over_e(m2[:, :]), ALU.is_equal))
            settled()
            step(dve.tensor_tensor(t3[:, :, :], t3[:, :, :], over_t(rev[:, :]), ALU.mult))
            settled()
            step(dve.tensor_reduce(k2[:, :], t3[:, :, :], AX_X, ALU.max))
            step(dve.tensor_scalar(m0[:, :], m2[:, :], 0.0, float(E), ALU.is_le, ALU.mult))
            settled()
            step(dve.tensor_tensor(m0[:, :], m0[:, :], k2[:, :], ALU.add))
            settled()
            step(dve.tensor_tensor(m0[:, :], m0[:, :], k1[:, :], ALU.min))
            settled()
            dve.tensor_tensor(chosen[:, 0:T, :], over_t(rev[:, :]), over_e(m0[:, :]), ALU.is_equal).then_inc(chosen_ready, 1)
            dve.wait_ge(chosen_ready, 1)
            step(dve.tensor_tensor(t3[:, :, :], chosen[:, 0:T, :], lg[:, :, :], ALU.mult))
            settled()
            step(dve.tensor_reduce(gw[:, :], t3[:, :, :], AX_X, ALU.add))
            settled()
            step(dve.tensor_copy(rows[:, :, :, D], mv2[:, :, 0].rearrange("p (b i) -> p b i", b=B)))
            dve.tensor_tensor(rows[:, :, :, D + 1], gw[:, :].rearrange("p (b i) -> p b i", b=B),
                              rstd2[:, :].rearrange("p (b i) -> p b i", b=B), ALU.mult).then_inc(rows_ready, 1)
            rank = bank[1][:, 0:(T + 1) * E].rearrange("p (t e) -> p t e", e=E)
            dve.wait_ge(rank_ps, 1)
            step(dve.tensor_tensor(cmp8[:, :, :], over_e(rank[:, T, :], T), over_t(thr[:, 0:T], E), ALU.is_gt))
            settled()
            step(dve.tensor_reduce(ntile[:, :], cmp8[:, :, :], AX_X, ALU.add))
            settled()
            step(dve.tensor_tensor_scan(upto[:, :], ones_e[:, :], ntile[:, :], 0.0, ALU.mult, ALU.add))
            settled()
            step(dve.tensor_tensor(first[:, :], upto[:, :], ntile[:, :], ALU.subtract))
            settled()
            step(dve.scalar_tensor_tensor(out=t3[:, :, :], in0=over_t(first[:, :]), scalar=float(P), in1=rank[:, 0:T, :],
                                          op0=ALU.mult, op1=ALU.add))
            settled()
            step(dve.tensor_tensor(t3[:, :, :], t3[:, :, :], chosen[:, 0:T, :], ALU.mult))
            settled()
            step(dve.tensor_reduce(pos[:, :], t3[:, :, :], AX_X, ALU.add))
            settled()
            step(dve.tensor_tensor(ge[:, :, :], over_e(pos[:, :], J + 1), over_t(thr[:, :]), ALU.is_ge))
            settled()
            step(dve.tensor_reduce(nge[:, :], ge[:, :, :], AX_X, ALU.add))
            step(dve.tensor_tensor(hit[:, :, 1, :], ge[:, :, 0:J], ge[:, :, 1:J + 1], ALU.subtract))
            settled()
            step(dve.scalar_tensor_tensor(out=lo[:, :], in0=nge[:, :], scalar=-float(P), in1=pos[:, :], op0=ALU.mult, op1=ALU.add))
            settled()
            for t in range(T):
                step(dve.tensor_scalar(lo_hot[:, t, :], lo_iota[:, :], lo[:, t:t + 1], None, ALU.is_equal))
            dve.tensor_tensor(hit[:, :, 0, :], hit[:, :, 1, :], over_e(token[:, :, :].rearrange("p b i -> p (b i)"), J),
                              ALU.mult).then_inc(hot_ready, 1)
            step(dve.tensor_tensor(cmpj[:, :, :], over_t(upto[0:1, :], J), over_e(jot[:, :]), ALU.is_le))
            settled()
            step(dve.tensor_reduce(expert_f[:, :], cmpj[:, :, :], AX_X, ALU.add))
            settled()
            dve.tensor_scalar(expert_of[:, :], expert_f[:, :], float(E - 1), None, ALU.min).then_inc(expert_ready, 1)
            dve.wait_ge(slot_ps, 1)
            step(dve.tensor_copy(src_row[:, :], bank[2][:, 0:J]))
            step(dve.tensor_scalar(emptyv[:, :], bank[2][:, J:2 * J], -BIG, BIG, ALU.mult, ALU.add))
            settled()
            dve.tensor_tensor(dst_row[:, :], emptyv[:, :], bank[2][:, 0:J], ALU.add).then_inc(slots_ready, 1)

            def scale_rows(j, k, turn):
                g = gat[:, bass.ds(j, 1), :].rearrange("p j c -> p (j c)")
                dve.wait_ge(gathered[k], turn)
                dve.tensor_scalar(xs[:, :], g[:, 0:D], g[:, D:D + 1], g[:, D + 1:D + 2], ALU.subtract,
                                  ALU.mult).then_inc(xs_ready, 1)

            def copy_xsT(j):
                dve.wait_ge(xsT_ps, j + 1)
                dve.tensor_copy(xsT[:, :], bank[3][:, 0:P]).then_inc(xsT_ready, 1)

            def copy_hT(j):
                dve.wait_ge(hT_ps, j + 1)
                dve.tensor_copy(hT[:, :, :], bank[5][:, :].rearrange("p (c q) -> p c q", c=C)).then_inc(hT_ready, 1)

            def add_residual(j):
                dve.wait_ge(y_ps, j + 1)
                dve.tensor_tensor(y_sb[:, bass.ds(j, 1), :].rearrange("p j d -> p (j d)"), bank[6][:, 0:D],
                                  gat[:, bass.ds(j, 1), 0:D].rearrange("p j d -> p (j d)"), ALU.add).then_inc(y_ready, 1)

            scale_rows(0, 0, 16)
            copy_xsT(0)
            scale_rows(1, 1, 16)
            copy_xsT(1)
            copy_hT(0)
            with dve.Fori(0, J // RING - 1) as m:
                for k in range(RING):
                    j = m * RING + 1 + k
                    scale_rows(j + 1, (k + 2) % RING, (m + 1 + (k + 2) // RING) * 16)
                    copy_xsT(j + 1)
                    add_residual(j - 1)
                    copy_hT(j)
            scale_rows(J - 1, (J - 1) % RING, J // RING * 16)
            copy_xsT(J - 1)
            add_residual(J - 3)
            copy_hT(J - 2)
            add_residual(J - 2)
            copy_hT(J - 1)
            add_residual(J - 1)

        @block.tensor
        def _(pe):
            pe.wait_ge(consts_ready, 1)
            pe.wait_ge(ctx_loaded, 16)
            for b in range(B):
                ins = pe.transpose(bank[0][:, b * SKV:(b + 1) * SKV], ctx_sb[:, b, :], ident[0:SKV, 0:SKV])
            ins.then_inc(prep_ps, 1)
            pe.wait_ge(wq_loaded, 16)
            pe.transpose(bank[1][:, 0:P], wq_sb[:, :], ident[:, :]).then_inc(prep_ps, 1)
            pe.wait_ge(wk_loaded, 16)
            pe.wait_ge(prep_sb, 1)
            pe.matmul(bank[2][:, 0:B * SKV], wk_sb[:, :], ctxT[:, :, :].rearrange("p b s -> p (b s)"),
                      start=True, stop=True).then_inc(prep_ps, 1)
            pe.wait_ge(prep_sb, 3)
            kT_all = kT[:, :, :].rearrange("p b s -> p (b s)")
            pe.matmul(bank[3][:, 0:B * SKV], wqT[:, :], kT_all, start=True, stop=True).then_inc(prep_ps, 1)
            pe.wait_ge(wide_ready, 1)
            pe.matmul(bank[4][:, 0:B * SKV], bq_wide[:, :], kT_all, start=True, stop=True).then_inc(prep_ps, 1)
            pe.wait_ge(wv_loaded, 32)
            pe.wait_ge(consts_ready, 2)
            for b in range(B):
                o = bank[5][0:SKV, b * D:(b + 1) * D]
                pe.matmul(o, ctxT[:, b, :], wv_sb[:, :], start=True, stop=False)
                ins = pe.matmul(o, ones_row[:, 0:SKV], bv_sb[:, :], start=False, stop=True)
            ins.then_inc(prep_ps, 1)

            def transpose_tiles(src, b, done, ready):
                pe.wait_ge(xn_ready, ready)
                for i in range(I):
                    ins = pe.transpose(bank[6 + b][:, i * P:(i + 1) * P], src[:, b, i], ident[:, :])
                ins.then_inc(done, 1)

            for b in range(B):
                transpose_tiles(xn, b, xnT_ps, b + 1)
                pe.wait_ge(prep_sb, 4)
                pe.wait_ge(xnT_ready, b + 1)
                for i in range(I):
                    ins = pe.matmul(bank[b][:, i * SKV:(i + 1) * SKV], xnT[:, b, i], score_w[:, b], start=True, stop=True)
                ins.then_inc(s_ps, 1)
            for b in range(B):
                pe.wait_ge(p_ready, I * (b + 1))
                for i in range(I):
                    ins = pe.transpose(bank[2 + b][0:SKV, i * P:(i + 1) * P], p_sb[:, b, i], ident[:, :])
                ins.then_inc(pT_ps, 1)
                pe.wait_ge(prep_sb, 6)
                pe.wait_ge(pT_ready, b + 1)
                for i in range(I):
                    ins = pe.matmul(bank[4 + b][:, i * D:(i + 1) * D], pT[:, b, i], v_sb[:, b], start=True, stop=True)
                ins.then_inc(o_ps, 1)
            pe.wait_ge(gate_loaded, 32)
            for b in range(B):
                transpose_tiles(xn2, b, xnT_ps, B + b + 1)
                pe.wait_ge(xnT_ready, B + b + 1)
                for i in range(I):
                    t = b * I + i
                    ins = pe.matmul(bank[0][:, t * E:(t + 1) * E], xn2T[:, b, i], gw_sb[:, :], start=True, stop=True)
            ins.then_inc(logits_ps, 1)
            pe.wait_ge(chosen_ready, 1)
            rank = bank[1][:, 0:(T + 1) * E]
            for t in range(T):
                pe.matmul(rank[:, (t + 1) * E:], ones_bf[:, :],
                          chosen[:, t, :].unsqueeze(1).to_broadcast([P, T - t, E]),
                          start=t == 0, stop=False, skip_group_check=True)
            pe.matmul(rank, before[:, :], chosen[:, :, :].rearrange("p t e -> p (t e)"), start=False, stop=True,
                      skip_group_check=True).then_inc(rank_ps, 1)
            pe.wait_ge(hot_ready, 1)
            for t in range(T):
                ins = pe.matmul(bank[2][:, 0:2 * J], lo_hot[:, t, :], hit[:, t].rearrange("p a j -> p (a j)"),
                                start=t == 0, stop=t == T - 1)
            ins.then_inc(slot_ps, 1)

            pe.wait_ge(bias_ready, 16)
            pe.wait_ge(experts_loaded, 64)
            pe.wait_ge(expert_ready, 1)

            def turn_x(j):
                pe.wait_ge(xs_ready, j + 1)
                pe.transpose(bank[3][:, 0:P], xs[:, :], ident[:, :]).then_inc(xsT_ps, 1)

            def layer1(j, e):
                w = w1_sb[:, bass.ds(e, 1), :].rearrange("p e h -> p (e h)")
                bias = bias_sb[:, bass.ds(e * H, H)]
                pe.wait_ge(xsT_ready, j + 1)
                pe.matmul(bank[4][:, :], xsT[:, :], w, start=True, stop=False)
                pe.matmul(bank[4][:, :], ones_bf[0:3, :], bias, start=False, stop=True).then_inc(h_ps, 1)

            def turn_h(j):
                pe.wait_ge(h_ready, j + 1)
                for c in range(C):
                    ins = pe.transpose(bank[5][:, c * P:(c + 1) * P], h_sb[:, c, :], ident[:, :])
                ins.then_inc(hT_ps, 1)

            def layer2(j, e):
                ws = [w2_sb[:, bass.ds(e, 1), c, :].rearrange("p e d -> p (e d)") for c in range(C)]
                bias = bias_sb[:, bass.ds(e * D + E * H, D)]
                pe.wait_ge(hT_ready, j + 1)
                for c in range(C):
                    pe.matmul(bank[6][:, 0:D], hT[:, c, :], ws[c], start=c == 0, stop=False)
                pe.matmul(bank[6][:, 0:D], ones_bf[0:3, :], bias, start=False, stop=True).then_inc(y_ps, 1)

            def expert(j):
                return pe.value_load(expert_of[0:1, bass.ds(j, 1)], min_val=0, max_val=E - 1)

            turn_x(0)
            layer1(0, expert(0))
            turn_x(1)
            turn_h(0)
            with pe.Fori(1, J - 1) as j:
                layer1(j, expert(j))
                turn_x(j + 1)
                layer2(j - 1, expert(j - 1))
                turn_h(j)
            layer1(J - 1, expert(J - 1))
            layer2(J - 2, expert(J - 2))
            turn_h(J - 1)
            layer2(J - 1, expert(J - 1))


_INS = ['x', 'ctx_1024', 'L0_xattn_Wq', 'L0_xattn_bq', 'L0_xattn_Wk', 'L0_xattn_bk', 'L0_xattn_Wv', 'L0_xattn_bv',
        'L0_ffn_gate_w', 'L0_ffn_gate_b', 'L0_ffn_w1', 'L0_ffn_b1', 'L0_ffn_w2', 'L0_ffn_b2']


def kernel(**inputs):
    import numpy as _np
    import concourse.bacc as _bacc
    from concourse import mybir as _mybir
    from concourse.bass_utils import run_bass_kernel_spmd as _run

    nc = _bacc.Bacc("TRN2", target_bir_lowering=False, num_devices=1)
    arrays, args = {}, []
    for name in _INS:
        a = _np.ascontiguousarray(inputs[name])
        arrays[f"in_{name}"] = a
        args.append(nc.dram_tensor(f"in_{name}", a.shape, _mybir.dt.from_np(a.dtype), kind="ExternalInput").ap())
    shape = inputs['x'].shape
    args.append(nc.dram_tensor("out_0", shape, _mybir.dt.float32, kind="ExternalOutput").ap())
    xattn_moe_kernel(nc, *args)
    r = _run(nc, [arrays], core_ids=[0])
    return r.results[0]["out_0"]
```

```python
from contextlib import ExitStack

import concourse.bass as bass
from concourse import mybir

F32 = mybir.dt.float32
BF16 = mybir.dt.bfloat16
F16 = mybir.dt.float16
U32 = mybir.dt.uint32
I32 = mybir.dt.int32
ALU = mybir.AluOpType
ACT = mybir.ActivationFunctionType
AX_X = mybir.AxisListType.X

P = 128
EPS = 1e-5
LOG_TINY = -87.33654
BIG = 4096.0


def xattn_moe_kernel(nc, x, ctx_in, Wq, bq, Wk, bk, Wv, bv, gate_w, gate_b, w1, b1, w2, b2, out):
    B, SQ, D = x.shape
    SKV = ctx_in.shape[1]
    E, _, H = w1.shape
    N = B * SQ
    I = SQ // P
    T = B * I
    S = E - 1
    J = S + T
    C = H // P
    SCALE = 1.0 / float(D) ** 0.5
    EXT = D + E
    NB2 = E * D // P
    ROW = EXT + 2
    RING = 8
    LOG_I, LOG_T, LOG_SQ = (n.bit_length() - 1 for n in (I, T, SQ))
    assert D == P and H == C * P and SKV <= P and B == 2 and E == 8 and T == S + 1
    assert (I, T, SQ) == (1 << LOG_I, 1 << LOG_T, 1 << LOG_SQ)

    b2_dram = nc.dram_tensor("b2_parts", [3, E * D], BF16).ap()
    rows_dram = nc.dram_tensor("token_rows", [N, ROW], F32).ap()

    with ExitStack() as ctx:
        def sb(name, shape, dt=F32):
            return ctx.enter_context(nc.sbuf_tensor(name, shape, dt))

        def sem(name):
            return ctx.enter_context(nc.semaphore(name))

        bank = [ctx.enter_context(nc.psum_tensor(f"bank{i}", [P, 512], F32)) for i in range(8)]

        x_sb = sb("x_sb", [P, B, I, EXT])
        ctx_sb = sb("ctx_sb", [SKV, B, D])
        wq_sb, wk_sb, wv_sb = sb("wq_sb", [P, D]), sb("wk_sb", [P, D]), sb("wv_sb", [P, D])
        bq_sb, bk_sb, bv_sb = sb("bq_sb", [P, 1]), sb("bk_sb", [P, 1]), sb("bv_sb", [1, D])
        bv_col = sb("bv_col", [P, 1])
        gw_sb, gb_sb = sb("gw_sb", [P, E]), sb("gb_sb", [P, E])
        w1_sb = sb("w1_sb", [P, S, H])
        w2_sb = sb("w2_sb", [P, S, C, D])
        b1_sb, b1T = sb("b1_sb", [E * C, P]), sb("b1T", [P, E, C])
        w1_more, w2_more = sb("w1_more", [P, T, H]), sb("w2_more", [P, T, C, D])
        b1_more, b2_more = sb("b1_more", [P, T, C]), sb("b2_more", [3, T, D], BF16)
        b2_sb = sb("b2_sb", [P, NB2])
        ident = sb("ident", [P, P])
        centre = sb("centre", [P, P])
        before = sb("before", [P, P], BF16)
        ones_bf = sb("ones_bf", [P, P], BF16)
        ones_row = sb("ones_row", [1, P])
        half = sb("half", [P, I])
        lo_iota = sb("lo_iota", [P, P], F16)
        e_iota = sb("e_iota", [P, E])
        j_iota = sb("j_iota", [P, J])
        j_less_e = sb("j_less_e", [1, T, E])
        thr = sb("thr", [P, T])
        skip0 = sb("skip0", [1, T + 1, E], BF16)
        token = sb("token", [P, T])
        minus_e = sb("minus_e", [P, E + 1])
        warm = sb("warm", [1, 1])
        ctxT, wqT = sb("ctxT", [P, B, SKV]), sb("wqT", [P, P])
        kT = sb("kT", [P, B, SKV])
        score_w = sb("score_w", [P, B, SKV + E])
        bq_share = sb("bq_share", [P, 1])
        vT, v_sb = sb("vT", [P, B, SKV]), sb("v_sb", [SKV, B, EXT])
        stats, mv, varp, rstd = sb("stats", [P, T, 6]), sb("mv", [P, T, 2]), sb("varp", [P, T]), sb("rstd", [P, T])
        std = sb("std", [P, T])
        shift, mean_n = sb("shift", [P, T]), sb("mean_n", [P, T])
        xn, xT = sb("xn", [P, B, I, D]), sb("xT", [P, B, I, P])
        p_sb, pn_sb = sb("p_sb", [P, B, I, SKV]), sb("pn_sb", [P, B, I, SKV])
        smax, nsmax, ssum, sinv = (sb(n, [P, B, I]) for n in ("smax", "nsmax", "ssum", "sinv"))
        pT = sb("pT", [SKV, B, I, P])
        rows = sb("rows", [P, B, I, ROW])
        stats2, mv2, varp2, rstd2 = (sb("stats2", [P, T, 6]), sb("mv2", [P, T, 2]), sb("varp2", [P, T]),
                                     sb("rstd2", [P, T]))
        zr = sb("zr", [P, T, E])
        z, zd, ez = sb("z", [P, T, E]), sb("zd", [P, T, E]), sb("ez", [P, T, E])
        top, top_at = sb("top", [P, T, 8]), sb("top_at", [P, T, 8], U32)
        gap, second, pick = sb("gap", [P, T]), sb("second", [P, T]), sb("pick", [P, T])
        first_best, weight, weighted = (sb(n, [P, T]) for n in ("first_best", "weight", "weighted"))
        esum, inv_esum = sb("esum", [P, T]), sb("inv_esum", [P, T])
        r3, f3 = sb("r3", [P, T, E]), sb("f3", [P, T, E])
        chosen = sb("chosen", [P, T + 1, E], BF16)
        ntile, first = sb("ntile", [P, E + 1]), sb("first", [P, E + 1])
        cmp8, cmpj = sb("cmp8", [P, E, T]), sb("cmpj", [1, T, E])
        expert_f = sb("expert_f", [1, T])
        table = sb("table", [1, T + 1], I32)
        rtok, lo, hi = sb("rtok", [P, T], I32), sb("lo", [P, T], I32), sb("hi", [P, T], I32)
        ftok, tile_of = sb("ftok", [P, T]), sb("tile_of", [P, T])
        own_tile, from_own = sb("own_tile", [P, T]), sb("from_own", [P, T])
        moved = sb("moved", [P, T])
        lo_f, away = sb("lo_f", [P, T]), sb("away", [P, T, P], F16)
        hit = sb("hit", [P, T, 2, J], F16)
        lo_hot = sb("lo_hot", [P, T, P], F16)
        src_row, dst_row = sb("src_row", [P, J], U32), sb("dst_row", [P, J], U32)
        emptyv = sb("emptyv", [P, J])
        row_int, part_p, part_b, part_i, part_pb = (sb(n, [P, J], I32) for n in ("row_int", "part_p", "part_b", "part_i", "part_pb"))
        part_ie = sb("part_ie", [P, J])
        part = sb("part", [P, 3, NB2], BF16)
        rest = sb("rest", [P, 2, NB2])
        b2_rows = sb("b2_rows", [3, E * D], BF16)
        gat = sb("gat", [P, J, ROW])
        xs, xsT = sb("xs", [P, 2, D]), sb("xsT", [P, 2, P])
        hT = sb("hT", [P, 2, C, P])
        y_sb = sb("y_sb", [P, J, D])

        x_loaded = [sem(f"x_loaded{b}") for b in range(B)]
        ctx_loaded, wq_loaded, wk_loaded, wv_loaded = (sem(n) for n in (
            "ctx_loaded", "wq_loaded", "wk_loaded", "wv_loaded"))
        bk_loaded, gate_loaded, experts_loaded, b1_loaded = (sem(n) for n in (
            "bk_loaded", "gate_loaded", "experts_loaded", "b1_loaded"))
        bq_share_ready = sem("bq_share_ready")
        bq_loaded, gw_loaded, bv_col_loaded = sem("bq_loaded"), sem("gw_loaded"), sem("bv_col_loaded")
        b2_loaded, b2_stored, b2_ready = sem("b2_loaded"), sem("b2_stored"), sem("b2_ready")
        pool_chain, dve_chain = sem("pool_chain"), sem("dve_chain")
        ident_ready, consts_ready, centre_ready, ones_bf_ready, ones_row_ready, warm_ready = (sem(n) for n in (
            "ident_ready", "consts_ready", "centre_ready", "ones_bf_ready", "ones_row_ready", "warm_ready"))
        ctxT_ps, wqT_ps, kT_ps, sw_ps, vT_ps, v_ps, gwc_ps = (sem(n) for n in (
            "ctxT_ps", "wqT_ps", "kT_ps", "sw_ps", "vT_ps", "v_ps", "gwc_ps"))
        ctxT_ready, wqT_ready, kT_ready, gwc_ready, score_w_ready, vT_ready, v_ready = (sem(n) for n in (
            "ctxT_ready", "wqT_ready", "kT_ready", "gwc_ready", "score_w_ready", "vT_ready", "v_ready"))
        var_ready, rstd_ready, shift_ready = sem("var_ready"), sem("rstd_ready"), sem("shift_ready")
        act_xn_ready, dve_xn_ready, xT_ps, xT_ready = sem("act_xn_ready"), sem("dve_xn_ready"), sem("xT_ps"), sem("xT_ready")
        s_ps, max_ready, p_ready, pT_ps, pT_ready = (sem(n) for n in (
            "s_ps", "max_ready", "p_ready", "pT_ps", "pT_ready"))
        pn_ready, x1_ps, stats_ready = sem("pn_ready"), sem("x1_ps"), sem("stats_ready")
        xg_ready, x1_ready, zd_ready, ez_ready = (sem(n) for n in ("xg_ready", "x1_ready", "zd_ready", "ez_ready"))
        pick_ready, weight_ready, esum_ready = sem("pick_ready"), sem("weight_ready"), sem("esum_ready")
        lo_f_ready, away_ready, act_hot_ready = sem("lo_f_ready"), sem("away_ready"), sem("act_hot_ready")
        lo_ready, pool_hot_ready, means_ready = sem("lo_ready"), sem("pool_hot_ready"), sem("means_ready")
        chosen_ready, rank_ps, hot_ready, slot_ps = (sem(n) for n in (
            "chosen_ready", "rank_ps", "hot_ready", "slot_ps"))
        parts_ready, rows_ready, rows_stored = sem("parts_ready"), sem("rows_ready"), sem("rows_stored")
        src_ready, dst_ready, table_ready = sem("src_ready"), sem("dst_ready"), sem("table_ready")
        gathered = [sem(f"gathered{k}") for k in range(RING)]
        more_loaded = [sem(f"more_loaded{k}") for k in range(T)]
        late_stored = [sem(f"late_stored{j}") for j in range(T, J)]
        xs_ready, xsT_ps, xsT_ready, y_ps, y_ready, y_stored = (sem(n) for n in (
            "xs_ready", "xsT_ps", "xsT_ready", "y_ps", "y_ready", "y_stored"))
        act_h_ps, act_h_ready, dve_h_ps, dve_h_ready = (sem(n) for n in (
            "act_h_ps", "act_h_ready", "dve_h_ps", "dve_h_ready"))

        x_dram = x.rearrange("b (p i) d -> b p i d", i=I)
        rows_store = rows_dram.rearrange("(p t) c -> p t c", t=T)
        out_dram = out.rearrange("b s d -> (b s) d")

        s_bank, pT_bank, xT_bank = [bank[0], bank[1]], [bank[2], bank[3]], [bank[6], bank[7]]

        def s_tile(b, i, n=SKV + E):
            return s_bank[b][:, i * (SKV + E):i * (SKV + E) + n]

        def x1_tile(b, i):
            return bank[4 + 2 * b + i // 2][:, (i % 2) * EXT:(i % 2 + 1) * EXT]

        def w1_of(j, c):
            return (w1_sb[:, j] if j < S else w1_more[:, j - S])[:, c * P:(c + 1) * P]

        def w2_of(j, c):
            return w2_sb[:, j, c, :] if j < S else w2_more[:, j - S, c, :]

        def b1_of(j, c):
            return b1T[:, j + 1, c:c + 1] if j < S else b1_more[:, j - S, c:c + 1]

        def b2_of(j):
            return b2_rows[:, (j + 1) * D:(j + 2) * D] if j < S else b2_more[:, j - S, :]

        xsT_bank = [bank[6], bank[0]]
        act_h_bank, dve_h_bank = [bank[4], bank[2]], [bank[5], bank[3]]
        y_bank = [bank[7], bank[1]]
        HALF = C // 2
        ACT_XN = 1
        POOL_HOT, ACT_HOT = 3, 2
        WARM = [28, 9, 0, 24, 0, 0, 0, 80, 44, 30, 2]

        def is_a_tile(eng, tiles, j):
            return eng.If(tiles > j)

        block = ctx.enter_context(nc.Block())

        @block.sync
        def _(sp):
            sp.dma_start(x_sb[:, 0, :, 0:D], x_dram[0]).then_inc(x_loaded[0], 16)
            sp.dma_start(x_sb[:, 1, :, 0:D], x_dram[1]).then_inc(x_loaded[1], 16)
            sp.dma_start(bk_sb[:, :], bk.rearrange("(d a) -> d a", a=1)).then_inc(bk_loaded, 16)
            sp.dma_start(bq_sb[:, :], bq.rearrange("(d a) -> d a", a=1)).then_inc(bq_loaded, 16)
            sp.dma_start(gw_sb[:, :], gate_w).then_inc(gw_loaded, 16)
            sp.dma_start(bv_col[:, :], bv.rearrange("(d a) -> d a", a=1)).then_inc(bv_col_loaded, 16)
            sp.dma_start(bv_sb[:, :], bv.rearrange("(a d) -> a d", a=1)).then_inc(wv_loaded, 16)
            sp.dma_start(gb_sb[:, :], gate_b.rearrange("(a e) -> a e", a=1).to_broadcast([P, E])).then_inc(gate_loaded, 16)
            sp.dma_start(b2_sb[:, :], b2.rearrange("e d -> (e d)").rearrange("(p f) -> p f", p=P)).then_inc(b2_loaded, 16)
            sp.dma_start(b1_sb[:, :], b1.rearrange("e (c q) -> (e c) q", q=P)).then_inc(b1_loaded, 16)
            for lo_e, hi_e in ((1, E // 2), (E // 2, E)):
                sp.dma_start(w1_sb[:, lo_e - 1:hi_e - 1], w1[lo_e:hi_e].rearrange("e d h -> d e h")).then_inc(experts_loaded, 16)
                for e in range(lo_e, hi_e):
                    sp.dma_start(w2_sb[:, e - 1], w2[e].rearrange("(c p) d -> p c d", p=P)).then_inc(experts_loaded, 16)
            sp.wait_ge(parts_ready, 1)
            sp.dma_start(b2_dram.rearrange("j (p f) -> p j f", p=P), part[:, :, :]).then_inc(b2_stored, 16)
            sp.wait_ge(b2_stored, 16)
            sp.dma_start(b2_rows[:, :], b2_dram).then_inc(b2_ready, 16)
            for b in range(B):
                sp.wait_ge(x1_ready, 2 * (b + 1))
                sp.dma_start(rows_store[:, b * I:(b + 1) * I, 0:EXT], rows[:, b, :, 0:EXT]).then_inc(rows_stored, 16)
            sp.wait_ge(means_ready, B)
            sp.wait_ge(rows_ready, 1)
            sp.dma_start(rows_store[:, :, EXT:], rows[:, :, :, EXT:].rearrange("p b i c -> p (b i) c")).then_inc(rows_stored, 16)
            sp.wait_ge(table_ready, 1)
            tiles = sp.value_load(table[0:1, T:T + 1], min_val=T, max_val=J)

            def fetch_weights(k):
                e = sp.value_load(table[0:1, k:k + 1], min_val=0, max_val=E - 1)
                here = more_loaded[k]
                sp.dma_start(w1_more[:, k, :], w1[bass.ds(e, 1)].rearrange("e d h -> d (e h)")).then_inc(here, 16)
                sp.dma_start(w2_more[:, k], w2[bass.ds(e, 1)].rearrange("e (c p) d -> p (e c) d", p=P)).then_inc(here, 16)
                sp.dma_start(b1_more[:, k, :], b1T[:, bass.ds(e, 1), :].rearrange("p e c -> p (e c)")).then_inc(here, 16)
                sp.dma_start(b2_more[:, k, :], b2_dram.rearrange("j (e d) -> j e d", e=E)[:, bass.ds(e, 1)]
                             .rearrange("j e d -> j (e d)")).then_inc(here, 16)

            sp.wait_ge(gathered[1], 16)
            fetch_weights(0)
            with ExitStack() as more:
                for j in range(T, J):
                    more.enter_context(sp.If(tiles > j))
                    fetch_weights(j - S)
            sp.wait_ge(y_stored, 16 * T)
            with ExitStack() as more:
                for j in range(T, J):
                    more.enter_context(sp.If(tiles > j))
                    sp.wait_ge(late_stored[j - T], 16)

        @block.gpsimd
        def _(pool):
            made = [0]

            def step(ins):
                made[0] += 1
                ins.then_inc(pool_chain, 1)

            step(pool.memset(ident[:, :], 0.0))
            pool.memset(ones_bf[:, :], 1.0).then_inc(ones_bf_ready, 1)
            pool.wait_ge(pool_chain, 1)
            pool.affine_select(out=ident[:, :], in_=ident[:, :], compare_op=ALU.not_equal, fill=1.0, base=0,
                               pattern=[[-1, P]], channel_multiplier=1).then_inc(ident_ready, 1)
            step(pool.memset(centre[:, :], -1.0 / D))
            pool.wait_ge(pool_chain, made[0])
            pool.affine_select(out=centre[:, :], in_=centre[:, :], compare_op=ALU.not_equal, fill=1.0 - 1.0 / D, base=0,
                               pattern=[[-1, P]], channel_multiplier=1).then_inc(centre_ready, 1)
            pool.memset(ones_row[:, :], 1.0).then_inc(ones_row_ready, 1)
            step(pool.memset(before[:, :], 1.0))
            step(pool.memset(half[:, :], -0.5))
            step(pool.memset(skip0[:, :, 1:], 0.0))
            step(pool.memset(skip0[:, :, 0:1], float(P)))
            pool.wait_ge(pool_chain, made[0])

            def inverse_root(src, dst, b, at):
                pool.wait_ge(var_ready, at)
                t = slice(b * I, (b + 1) * I)
                pool.tensor_tensor(dst[:, t], src[:, t], half[:, :], ALU.pow).then_inc(rstd_ready, 1)

            for b in range(B):
                inverse_root(varp, rstd, b, b + 1)
            pool.affine_select(out=before[:, :], in_=before[:, :], compare_op=ALU.is_gt, fill=0.0, base=0,
                               pattern=[[1, P]], channel_multiplier=-1)
            pool.memset(minus_e[:, :], -1.0)
            pool.memset(ntile[:, 0:1], 0.0)
            pool.memset(chosen[:, T, :], 0.0)
            for tensor, pattern, base, scale in ((lo_iota, [[1, P]], 0, 0), (e_iota, [[1, E]], 0, 0), (j_iota, [[1, J]], 0, 0),
                                                 (j_less_e, [[1, T], [-1, E]], S - 1, 0), (thr, [[P, T]], P, 0),
                                                 (token, [[1, T]], 0, T)):
                at = tensor[:, :, :] if tensor is j_less_e else tensor[:, :]
                last = pool.iota(at, pattern=pattern, base=base, channel_multiplier=scale,
                                 allow_small_or_imprecise_dtypes=True)
            last.then_inc(consts_ready, 1)
            pool.wait_ge(b2_loaded, 16)
            step(pool.tensor_copy(part[:, 0], b2_sb[:, :]))
            pool.wait_ge(pool_chain, made[0])
            step(pool.tensor_tensor(rest[:, 0], b2_sb[:, :], part[:, 0], ALU.subtract))
            pool.wait_ge(pool_chain, made[0])
            step(pool.tensor_copy(part[:, 1], rest[:, 0]))
            pool.wait_ge(pool_chain, made[0])
            step(pool.tensor_tensor(rest[:, 1], rest[:, 0], part[:, 1], ALU.subtract))
            pool.wait_ge(pool_chain, made[0])
            pool.tensor_copy(part[:, 2], rest[:, 1]).then_inc(parts_ready, 1)
            for b in range(B):
                inverse_root(varp2, rstd2, b, B + b + 1)
            pool.wait_ge(weight_ready, 1)
            step(pool.tensor_tensor(weighted[:, :], weight[:, :], rstd2[:, :], ALU.mult))
            pool.wait_ge(pool_chain, made[0])
            pool.wait_ge(esum_ready, 1)
            pool.tensor_tensor(rows[:, :, :, EXT + 1], weighted[:, :].rearrange("p (b i) -> p b i", b=B),
                               inv_esum[:, :].rearrange("p (b i) -> p b i", b=B), ALU.mult).then_inc(rows_ready, 1)
            pool.wait_ge(lo_ready, 1)
            for t in range(T - POOL_HOT, T):
                ins = pool.tensor_scalar(lo_hot[:, t, :], lo_iota[:, :], lo[:, t:t + 1], None, ALU.is_equal)
            ins.then_inc(pool_hot_ready, 1)

            def gather(j):
                pool.indirect_dma_start(gat[:, j, :], None, rows_dram,
                                        bass.IndirectOffsetOnAxis(src_row[:, j:j + 1], 0)).then_inc(gathered[j % RING], 16)

            def scatter(j):
                pool.wait_ge(y_ready, j + 1)
                pool.indirect_dma_start(out_dram, bass.IndirectOffsetOnAxis(dst_row[:, j:j + 1], 0), y_sb[:, j, :], None,
                                        bounds_check=N - 1, oob_is_err=False).then_inc(
                                            y_stored if j < T else late_stored[j - T], 16)

            pool.wait_ge(rows_stored, 16 * (B + 1))
            pool.wait_ge(src_ready, 1)
            for j in range(RING):
                gather(j)
            pool.wait_ge(table_ready, 1)
            tiles = pool.value_load(table[0:1, T:T + 1], min_val=T, max_val=J)
            pool.wait_ge(dst_ready, 1)

            def gather_ahead(j):
                pool.wait_ge(gathered[j % RING], 16 * (j // RING))
                gather(j)

            for j in range(J):
                ahead = j + RING
                if ahead < T:
                    gather_ahead(ahead)
                elif ahead < J:
                    with pool.If(tiles > ahead):
                        gather_ahead(ahead)
                if j < T:
                    scatter(j)
                else:
                    with pool.If(tiles > j):
                        scatter(j)

        @block.scalar
        def _(act):
            act.wait_ge(warm_ready, 1)
            act.activation(warm[:, :], warm[:, :], ACT.Exp)
            act.dma_start(ctx_sb[:, :, :], ctx_in.rearrange("b s d -> s b d")).then_inc(ctx_loaded, 16)
            act.dma_start(wk_sb[:, :], Wk).then_inc(wk_loaded, 16)
            act.dma_start(wq_sb[:, :], Wq).then_inc(wq_loaded, 16)
            act.dma_start(wv_sb[:, :], Wv).then_inc(wv_loaded, 16)
            act.wait_ge(ctxT_ps, 1)
            act.copy(ctxT[:, :, :], bank[0][:, 0:B * SKV].rearrange("p (b s) -> p b s", b=B)).then_inc(ctxT_ready, 1)
            act.wait_ge(bq_loaded, 16)
            act.mul(bq_share[:, :], bq_sb[:, :], 1.0 / D).then_inc(bq_share_ready, 1)
            act.wait_ge(kT_ps, 1)
            act.wait_ge(bk_loaded, 16)
            act.activation(kT[:, :, :], bank[2][:, 0:B * SKV].rearrange("p (b s) -> p b s", b=B), ACT.Identity,
                           bias=bk_sb[:, 0:1]).then_inc(kT_ready, 1)
            act.wait_ge(bq_share_ready, 1)
            act.wait_ge(wqT_ps, 1)
            act.activation(wqT[:, :], bank[1][:, 0:P], ACT.Identity, bias=bq_share[:, 0:1]).then_inc(wqT_ready, 1)

            def normalize(b):
                act.wait_ge(x_loaded[b], 16)
                act.wait_ge(shift_ready, b + 1)
                for i in range(ACT_XN):
                    t = b * I + i
                    act.activation(xn[:, b, i], x_sb[:, b, i, 0:D], ACT.Identity, bias=shift[:, t:t + 1],
                                   scale=rstd[:, t:t + 1]).then_inc(act_xn_ready, 1)

            normalize(0)
            act.wait_ge(sw_ps, 1)
            act.copy(score_w[:, :, 0:SKV], bank[3][:, 0:B * SKV].rearrange("p (b s) -> p b s", b=B)).then_inc(
                score_w_ready, 1)
            act.wait_ge(xT_ps, 1)
            act.copy(xT[:, 0], xT_bank[0][:, :].rearrange("p (i q) -> p i q", i=I)).then_inc(xT_ready, 1)
            normalize(1)
            act.wait_ge(vT_ps, 1)
            act.wait_ge(bv_col_loaded, 16)
            act.activation(vT[:, :, :], bank[2][:, 0:B * SKV].rearrange("p (b s) -> p b s", b=B), ACT.Identity,
                           bias=bv_col[:, 0:1]).then_inc(vT_ready, 1)
            act.wait_ge(xT_ps, 2)
            act.copy(xT[:, 1], xT_bank[1][:, :].rearrange("p (i q) -> p i q", i=I)).then_inc(xT_ready, 1)

            def exp_scores(b):
                act.wait_ge(max_ready, b + 1)
                for i in range(I):
                    act.activation(p_sb[:, b, i], s_tile(b, i, SKV), ACT.Exp, bias=nsmax[:, b, i:i + 1], scale=SCALE,
                                   accum_out=ssum[:, b, i:i + 1]).then_inc(p_ready, 1)

            exp_scores(0)
            exp_scores(1)
            act.wait_ge(pT_ps, 1)
            act.copy(pT[:, 0], pT_bank[0][0:SKV, :].rearrange("p (i q) -> p i q", i=I)).then_inc(pT_ready, 1)
            act.wait_ge(pT_ps, 2)
            act.copy(pT[:, 1], pT_bank[1][0:SKV, :].rearrange("p (i q) -> p i q", i=I)).then_inc(pT_ready, 1)
            for k in range(2 * B):
                act.wait_ge(stats_ready, k + 1)
                act.copy(rows[:, k // 2, k % 2 * 2:k % 2 * 2 + 2, 0:EXT],
                         bank[4 + k][:, 0:2 * EXT].rearrange("p (i d) -> p i d", i=2)).then_inc(x1_ready, 1)
            act.wait_ge(zd_ready, 1)
            act.activation(ez[:, :, :], zd[:, :, :], ACT.Exp).then_inc(ez_ready, 1)
            act.wait_ge(consts_ready, 1)
            act.wait_ge(lo_f_ready, 1)
            mine = range(T - POOL_HOT - ACT_HOT, T - POOL_HOT)
            for t in mine:
                act.activation(away[:, t, :], lo_iota[:, :], ACT.Abs, bias=lo_f[:, t:t + 1], scale=-1.0).then_inc(away_ready, 1)
            for k, t in enumerate(mine):
                act.wait_ge(away_ready, k + 1)
                act.activation(lo_hot[:, t, :], away[:, t, :], ACT.Relu, bias=1.0, scale=-1.0).then_inc(act_hot_ready, 1)

            def copy_xsT(j):
                act.wait_ge(xsT_ps, j + 1)
                act.copy(xsT[:, j % 2], xsT_bank[j % 2][:, 0:P]).then_inc(xsT_ready, 1)

            def relu_half(j):
                if j >= S:
                    act.wait_ge(more_loaded[j - S], 64)
                act.wait_ge(act_h_ps, j + 1)
                for c in range(HALF):
                    act.activation(hT[:, j % 2, c], act_h_bank[j % 2][:, c * P:(c + 1) * P], ACT.Relu,
                                   bias=b1_of(j, c)).then_inc(act_h_ready, 1)

            act.wait_ge(table_ready, 1)
            tiles = act.value_load(table[0:1, T:T + 1], min_val=T, max_val=J)

            def step_and_next(j):
                if j + 1 < T:
                    copy_xsT(j + 1)
                    relu_half(j)
                elif j + 1 < J:
                    with act.If(tiles > j + 1):
                        copy_xsT(j + 1)
                        relu_half(j)
                        step_and_next(j + 1)
                    with act.Else():
                        relu_half(j)
                else:
                    relu_half(j)

            copy_xsT(0)
            for j in range(T):
                step_and_next(j)

        @block.vector
        def _(dve):
            made = [0]

            def step(ins):
                made[0] += 1
                ins.then_inc(dve_chain, 1)
                return made[0]

            def settled(at=None):
                dve.wait_ge(dve_chain, made[0] if at is None else at)

            def over_e(a, n=E):
                return a.unsqueeze(2).to_broadcast([a.shape[0], a.shape[1], n])

            def over_t(a, n=T):
                return a.unsqueeze(1).to_broadcast([a.shape[0], n, a.shape[1]])

            def variance(src, b, stats, mv, varp):
                for i in range(I):
                    last = step(dve.bn_stats(stats[:, b * I + i, :], src(i)))
                for i in range(I):
                    settled(last - I + 1 + i)
                    step(dve.bn_aggr(mv[:, b * I + i, :], stats[:, b * I + i, :]))
                settled()
                t = slice(b * I, (b + 1) * I)
                dve.tensor_scalar(varp[:, t], mv[:, t, 1], EPS, None, ALU.add).then_inc(var_ready, 1)

            def row_shift(b):
                ts = slice(b * I, (b + 1) * I)
                dve.wait_ge(rstd_ready, b + 1)
                step(dve.tensor_tensor(mean_n[:, ts], mv[:, ts, 0], rstd[:, ts], ALU.mult))
                settled()
                dve.tensor_scalar(shift[:, ts], mean_n[:, ts], -1.0, 1.0, ALU.mult, ALU.add).then_inc(shift_ready, 1)

            def normalize(t):
                dve.tensor_scalar(xn[:, t // I, t % I], x_sb[:, t // I, t % I, 0:D], rstd[:, t:t + 1], shift[:, t:t + 1],
                                  ALU.mult, ALU.add).then_inc(dve_xn_ready, 1)

            dve.memset(warm[:, :], 0.0).then_inc(warm_ready, 1)
            for b in range(B):
                dve.wait_ge(x_loaded[b], 16)
                variance(lambda i: x_sb[:, b, i, 0:D], b, stats, mv, varp)
            row_shift(0)
            dve.wait_ge(shift_ready, 1)
            for t in range(ACT_XN, I):
                normalize(t)
            dve.wait_ge(gwc_ps, 1)
            dve.tensor_copy(score_w[:, :, SKV:], over_t(bank[4][:, 0:E], B)).then_inc(gwc_ready, 1)
            row_shift(1)
            std_at = step(dve.tensor_tensor(std[:, :], varp[:, :], rstd[:, :], ALU.mult))
            dve.wait_ge(shift_ready, 2)
            for t in range(I + ACT_XN, T):
                normalize(t)

            def row_max(b):
                dve.wait_ge(s_ps, b + 1)
                step(dve.tensor_reduce(smax[:, b], s_bank[b][:, 0:I * (SKV + E)].rearrange(
                    "p (i s) -> p i s", i=I)[:, :, 0:SKV], AX_X, ALU.max))
                settled(std_at)
                dve.tensor_tensor(x_sb[:, b, :, D:], s_bank[b][:, 0:I * (SKV + E)].rearrange(
                    "p (i s) -> p i s", i=I)[:, :, SKV:], over_e(std[:, b * I:(b + 1) * I]), ALU.mult).then_inc(xg_ready, 1)
                settled()
                dve.tensor_scalar(nsmax[:, b], smax[:, b], -SCALE, None, ALU.mult).then_inc(max_ready, 1)

            def softmax(b):
                dve.wait_ge(p_ready, I * (b + 1))
                step(dve.reciprocal(sinv[:, b], ssum[:, b]))
                settled()
                dve.tensor_tensor(pn_sb[:, b], p_sb[:, b], over_e(sinv[:, b], SKV), ALU.mult).then_inc(pn_ready, 1)

            row_max(0)
            dve.wait_ge(v_ps, 1)
            dve.tensor_copy(v_sb[:, :, :], bank[5][0:SKV, 0:B * EXT].rearrange("p (b d) -> p b d", b=B))
            dve.tensor_copy(b1T[:, :, :], bank[5][:, B * EXT:B * EXT + E * C].rearrange("p (e c) -> p e c", c=C)).then_inc(v_ready, 1)
            row_max(1)
            softmax(0)
            softmax(1)
            for b in range(B):
                for i in range(I):
                    if i % 2 == 0:
                        dve.wait_ge(x1_ps, 2 * b + i // 2 + 1)
                    ins = dve.bn_stats(stats2[:, b * I + i, :], x1_tile(b, i)[:, 0:D])
                    if i % 2 == 1:
                        ins.then_inc(stats_ready, 1)
                for i in range(I):
                    t = b * I + i
                    if i % 2 == 0:
                        dve.wait_ge(stats_ready, 2 * b + i // 2 + 1)
                    step(dve.bn_aggr(mv2[:, t, :], stats2[:, t, :]))
                settled()
                ts = slice(b * I, (b + 1) * I)
                dve.tensor_scalar(varp2[:, ts], mv2[:, ts, 1], EPS, None, ALU.add).then_inc(var_ready, 1)
                dve.tensor_copy(rows[:, b, :, EXT], mv2[:, ts, 0]).then_inc(means_ready, 1)

            dve.wait_ge(gate_loaded, 16)
            dve.wait_ge(consts_ready, 1)
            for b in range(B):
                dve.wait_ge(x1_ready, 2 * (b + 1))
                dve.wait_ge(rstd_ready, B + b + 1)
                ts = slice(b * I, (b + 1) * I)
                step(dve.tensor_tensor(zr[:, ts, :], rows[:, b, :, D:EXT], over_e(rstd2[:, ts], E), ALU.mult))
                settled()
                step(dve.tensor_tensor(z[:, ts, :], zr[:, ts, :], over_t(gb_sb[:, :], I), ALU.add))
                settled()
                for i in range(I):
                    step(dve.max(top[:, b * I + i, :], z[:, b * I + i, :]))
                settled()
                if b == B - 1:
                    step(dve.tensor_tensor(gap[:, :], top[:, :, 1], top[:, :, 0], ALU.subtract))
                for i in range(I):
                    t = b * I + i
                    index_at = step(dve.max_index(top_at[:, t, :], top[:, t, :], z[:, t, :]))
            dve.tensor_tensor(zd[:, :, :], top[:, :, :], over_e(top[:, :, 0], 8), ALU.subtract).then_inc(zd_ready, 1)
            settled(index_at)
            step(dve.scalar_tensor_tensor(out=second[:, :], in0=gap[:, :], scalar=LOG_TINY, in1=top_at[:, :, 1],
                                          op0=ALU.is_gt, op1=ALU.mult))
            settled()
            dve.tensor_tensor(pick[:, :], second[:, :], top_at[:, :, 0], ALU.max).then_inc(pick_ready, 1)
            dve.wait_ge(pick_ready, 1)
            dve.tensor_tensor(chosen[:, 0:T, :], over_t(e_iota[:, :]), over_e(pick[:, :]),
                              ALU.is_equal).then_inc(chosen_ready, 1)
            step(dve.tensor_scalar(own_tile[:, :], pick[:, :], -1.0, None, ALU.add))
            first_at = step(dve.tensor_tensor(first_best[:, :], second[:, :], top_at[:, :, 0], ALU.is_le))
            dve.wait_ge(ez_ready, 1)
            esum_at = step(dve.tensor_reduce(esum[:, :], ez[:, :, :], AX_X, ALU.add))
            settled(first_at)
            dve.tensor_tensor(weight[:, :], first_best[:, :], ez[:, :, 1], ALU.max).then_inc(weight_ready, 1)
            settled(esum_at)
            dve.reciprocal(inv_esum[:, :], esum[:, :]).then_inc(esum_ready, 1)
            rank = bank[2][:, 0:(T + 1) * E].rearrange("p (t e) -> p t e", e=E)
            dve.wait_ge(rank_ps, 1)
            step(dve.tensor_tensor(r3[:, :, :], rank[:, 0:T, :], chosen[:, 0:T, :], ALU.mult))
            step(dve.tensor_tensor(cmp8[:, :, :], over_e(rank[:, T, :], T), over_t(thr[:, :], E), ALU.is_gt))
            settled(made[0] - 1)
            with nc.allow_low_precision("ranks are whole numbers below 2**24"):
                step(dve.tensor_reduce(rtok[:, :], r3[:, :, :], AX_X, ALU.add))
            settled(made[0] - 1)
            step(dve.tensor_reduce(ntile[:, 1:], cmp8[:, :, :], AX_X, ALU.add))
            settled(made[0] - 1)
            dve.tensor_single_scalar(lo[:, :], rtok[:, :], P - 1, ALU.bitwise_and).then_inc(lo_ready, 1)
            hi_at = step(dve.tensor_single_scalar(hi[:, :], rtok[:, :], P.bit_length() - 1, ALU.arith_shift_right))
            settled(made[0] - 1)
            first_at = step(dve.tensor_tensor_scan(first[:, :], minus_e[:, :], ntile[:, :], float(E), ALU.add, ALU.add))
            settled(hi_at)
            dve.wait_ge(lo_ready, 1)
            dve.tensor_copy(lo_f[:, :], lo[:, :]).then_inc(lo_f_ready, 1)
            step(dve.tensor_tensor(from_own[:, :], own_tile[:, :], hi[:, :], ALU.add))
            settled(first_at)
            f3_at = step(dve.tensor_tensor(f3[:, :, :], chosen[:, 0:T, :], over_t(first[:, 0:E]), ALU.mult))
            settled(hi_at)
            dve.wait_ge(lo_ready, 1)
            for t in range(T - POOL_HOT - ACT_HOT):
                if t == 1:
                    settled(f3_at)
                    ftok_at = step(dve.tensor_reduce(ftok[:, :], f3[:, :, :], AX_X, ALU.add))
                if t == 2:
                    settled(ftok_at)
                    moved_at = step(dve.scalar_tensor_tensor(out=moved[:, :], in0=hi[:, :], scalar=0.0, in1=ftok[:, :],
                                                             op0=ALU.is_gt, op1=ALU.mult))
                step(dve.tensor_scalar(lo_hot[:, t, :], lo_iota[:, :], lo[:, t:t + 1], None, ALU.is_equal))
            settled(moved_at)
            tile_at = step(dve.tensor_tensor(tile_of[:, :], from_own[:, :], moved[:, :], ALU.add))
            settled(tile_at)
            step(dve.tensor_tensor(hit[:, :, 1, :], over_e(tile_of[:, :], J), over_t(j_iota[:, :]), ALU.is_equal))
            settled()
            dve.tensor_tensor(hit[:, :, 0, :], hit[:, :, 1, :], over_e(token[:, :], J), ALU.mult).then_inc(hot_ready, 1)
            cmpj_at = step(dve.tensor_tensor(cmpj[:, :, :], over_t(first[0:1, 1:]), j_less_e[:, :, :], ALU.is_le))
            dve.wait_ge(slot_ps, 1)
            dve.tensor_copy(src_row[:, :], bank[3][:, 0:J]).then_inc(src_ready, 1)
            row_at = step(dve.tensor_copy(row_int[:, :], bank[3][:, 0:J]))
            step(dve.tensor_scalar(emptyv[:, :], bank[3][:, J:2 * J], -BIG, BIG, ALU.mult, ALU.add))
            settled(cmpj_at)
            step(dve.tensor_reduce(expert_f[:, :], cmpj[:, :, :], AX_X, ALU.add))
            step(dve.tensor_scalar(table[:, T:T + 1], first[0:1, E:E + 1], float(E), None, ALU.add))
            settled(made[0] - 1)
            dve.tensor_scalar(table[:, 0:T], expert_f[:, :], float(E - 1), None, ALU.min).then_inc(table_ready, 1)
            settled(row_at)
            step(dve.tensor_scalar(part_p[:, :], row_int[:, :], LOG_T, LOG_I, ALU.arith_shift_right, ALU.arith_shift_left))
            step(dve.tensor_scalar(part_b[:, :], row_int[:, :], I, LOG_SQ - LOG_I, ALU.bitwise_and, ALU.arith_shift_left))
            step(dve.tensor_single_scalar(part_i[:, :], row_int[:, :], I - 1, ALU.bitwise_and))
            settled(made[0] - 1)
            step(dve.tensor_tensor(part_pb[:, :], part_p[:, :], part_b[:, :], ALU.add))
            settled(made[0] - 1)
            step(dve.tensor_tensor(part_ie[:, :], part_i[:, :], emptyv[:, :], ALU.add))
            settled()
            dve.tensor_tensor(dst_row[:, :], part_pb[:, :], part_ie[:, :], ALU.add).then_inc(dst_ready, 1)

            def scale_rows(j):
                dve.wait_ge(gathered[j % RING], 16 * (j // RING + 1))
                dve.tensor_scalar(xs[:, j % 2], gat[:, j, 0:D], gat[:, j, EXT:EXT + 1], gat[:, j, EXT + 1:EXT + 2], ALU.subtract,
                                  ALU.mult).then_inc(xs_ready, 1)

            def relu_half(j):
                if j >= S:
                    dve.wait_ge(more_loaded[j - S], 64)
                dve.wait_ge(dve_h_ps, j + 1)
                for c in range(HALF, C):
                    dve.tensor_scalar(hT[:, j % 2, c], dve_h_bank[j % 2][:, (c - HALF) * P:(c - HALF + 1) * P],
                                      b1_of(j, c), 0.0, ALU.add, ALU.max).then_inc(dve_h_ready, 1)

            def add_residual(j):
                dve.wait_ge(y_ps, j + 1)
                dve.tensor_tensor(y_sb[:, j, :], y_bank[j % 2][:, 0:D], gat[:, j, 0:D], ALU.add).then_inc(y_ready, 1)

            def step_and_next(j):
                if j + 1 < T:
                    scale_rows(j + 1)
                    relu_half(j)
                    if j:
                        add_residual(j - 1)
                elif j + 1 < J:
                    with dve.If(tiles > j + 1):
                        scale_rows(j + 1)
                        relu_half(j)
                        add_residual(j - 1)
                        step_and_next(j + 1)
                    with dve.Else():
                        finish(j)
                else:
                    finish(j)

            def finish(j):
                relu_half(j)
                add_residual(j - 1)
                add_residual(j)

            dve.wait_ge(table_ready, 1)
            tiles = dve.value_load(table[0:1, T:T + 1], min_val=T, max_val=J)
            scale_rows(0)
            for j in range(T):
                step_and_next(j)

        @block.tensor
        def _(pe):
            def keep_warm(n, to):
                for _ in range(n):
                    pe.matmul(to[:, 0:P], ones_bf[:, :], ones_bf[:, :], start=True, stop=True)

            pe.wait_ge(ones_bf_ready, 1)
            keep_warm(WARM[0], bank[7])
            pe.wait_ge(ident_ready, 1)
            pe.wait_ge(ctx_loaded, 16)
            for b in range(B):
                ins = pe.transpose(bank[0][:, b * SKV:(b + 1) * SKV], ctx_sb[:, b, :], ident[0:SKV, 0:SKV])
            ins.then_inc(ctxT_ps, 1)
            keep_warm(WARM[1], bank[7])
            pe.wait_ge(wk_loaded, 16)
            pe.wait_ge(ctxT_ready, 1)
            ctxT_all = ctxT[:, :, :].rearrange("p b s -> p (b s)")
            pe.matmul(bank[2][:, 0:B * SKV], wk_sb[:, :], ctxT_all, start=True, stop=True).then_inc(kT_ps, 1)
            pe.wait_ge(centre_ready, 1)
            pe.wait_ge(wq_loaded, 16)
            pe.matmul(bank[1][:, 0:P], wq_sb[:, :], centre[:, :], start=True, stop=True).then_inc(wqT_ps, 1)
            pe.wait_ge(gw_loaded, 16)
            pe.matmul(bank[4][:, 0:E], centre[:, :], gw_sb[:, :], start=True, stop=True).then_inc(gwc_ps, 1)
            def transpose_x(b):
                for i in range(I):
                    if i < ACT_XN:
                        pe.wait_ge(act_xn_ready, b * ACT_XN + i + 1)
                    else:
                        pe.wait_ge(dve_xn_ready, b * (I - ACT_XN) + i - ACT_XN + 1)
                    ins = pe.transpose(xT_bank[b][:, i * P:(i + 1) * P], xn[:, b, i], ident[:, :])
                ins.then_inc(xT_ps, 1)

            keep_warm(WARM[10], bank[7])
            pe.wait_ge(kT_ready, 1)
            pe.wait_ge(wqT_ready, 1)
            pe.matmul(bank[3][:, 0:B * SKV], wqT[:, :], kT[:, :, :].rearrange("p b s -> p (b s)"),
                      start=True, stop=True).then_inc(sw_ps, 1)
            transpose_x(0)

            def scores(b):
                pe.wait_ge(xT_ready, b + 1)
                for i in range(I):
                    ins = pe.matmul(s_tile(b, i), xT[:, b, i], score_w[:, b], start=True, stop=True)
                ins.then_inc(s_ps, 1)

            pe.wait_ge(wv_loaded, 32)
            pe.matmul(bank[2][:, 0:B * SKV], wv_sb[:, :], ctxT_all, start=True, stop=True).then_inc(vT_ps, 1)
            v_bank = bank[5]

            def values(b):
                o = v_bank[0:SKV, b * EXT:b * EXT + D]
                pe.matmul(o, ctxT[:, b, :], wv_sb[:, :], start=True, stop=False)
                pe.matmul(o, ones_row[:, 0:SKV], bv_sb[:, :], start=False, stop=True)

            pe.wait_ge(ones_row_ready, 1)
            values(0)
            pe.wait_ge(gwc_ready, 1)
            pe.wait_ge(score_w_ready, 1)
            scores(0)
            transpose_x(1)
            values(1)
            pe.wait_ge(vT_ready, 1)
            for b in range(B):
                pe.matmul(v_bank[0:SKV, b * EXT + D:(b + 1) * EXT], vT[:, b, :], score_w[:, b, SKV:],
                          start=True, stop=True)
            pe.wait_ge(b1_loaded, 16)
            pe.transpose(v_bank[:, B * EXT:B * EXT + E * C], b1_sb[:, :], ident[0:E * C, 0:E * C]).then_inc(v_ps, 1)
            scores(1)

            def transpose_p(b):
                pe.wait_ge(pn_ready, b + 1)
                for i in range(I):
                    ins = pe.transpose(pT_bank[b][0:SKV, i * P:(i + 1) * P], pn_sb[:, b, i], ident[:, :])
                ins.then_inc(pT_ps, 1)

            def add_x(b):
                pe.wait_ge(xg_ready, b + 1)
                for i in range(I):
                    pe.matmul(x1_tile(b, i), ident[:, :], x_sb[:, b, i, :], start=i % 2 == 0, stop=False,
                              skip_group_check=True)

            def attend(b):
                pe.wait_ge(pT_ready, b + 1)
                for i in range(I):
                    ins = pe.matmul(x1_tile(b, i), pT[:, b, i], v_sb[:, b], start=False, stop=True, skip_group_check=True)
                    if i % 2 == 1:
                        ins.then_inc(x1_ps, 1)

            pe.wait_ge(v_ready, 1)
            add_x(0)
            keep_warm(WARM[4], bank[2])
            transpose_p(0)
            add_x(1)
            keep_warm(WARM[5], bank[0])
            transpose_p(1)
            attend(0)
            attend(1)
            keep_warm(WARM[7], bank[2])
            pe.wait_ge(consts_ready, 1)
            pe.wait_ge(chosen_ready, 1)
            rank = bank[2][:, 0:(T + 1) * E]
            pe.matmul(rank, ones_bf[0:1, :], skip0[:, :, :].rearrange("a t e -> a (t e)"), start=True, stop=False,
                      skip_group_check=True)
            for t in range(T):
                pe.matmul(rank[:, (t + 1) * E:], ones_bf[:, :],
                          chosen[:, t, :].unsqueeze(1).to_broadcast([P, T - t, E]),
                          start=False, stop=False, skip_group_check=True)
            pe.matmul(rank, before[:, :], chosen[:, :, :].rearrange("p t e -> p (t e)"), start=False, stop=True,
                      skip_group_check=True).then_inc(rank_ps, 1)
            keep_warm(WARM[8], bank[0])
            pe.wait_ge(hot_ready, 1)
            pe.wait_ge(pool_hot_ready, 1)
            pe.wait_ge(act_hot_ready, ACT_HOT)
            for t in range(T):
                ins = pe.matmul(bank[3][:, 0:2 * J], lo_hot[:, t, :], hit[:, t].rearrange("p a j -> p (a j)"),
                                start=t == 0, stop=t == T - 1)
            ins.then_inc(slot_ps, 1)

            def turn_x(j):
                pe.wait_ge(xs_ready, j + 1)
                pe.transpose(xsT_bank[j % 2][:, 0:P], xs[:, j % 2], ident[:, :]).then_inc(xsT_ps, 1)

            def layer1(j):
                if j >= S:
                    pe.wait_ge(more_loaded[j - S], 64)
                pe.wait_ge(xsT_ready, j + 1)
                for c in range(C):
                    to, at, done = ((act_h_bank, c, act_h_ps) if c < HALF else (dve_h_bank, c - HALF, dve_h_ps))
                    ins = pe.matmul(to[j % 2][:, at * P:(at + 1) * P], w1_of(j, c), xsT[:, j % 2], start=True, stop=True)
                    if c in (HALF - 1, C - 1):
                        ins.then_inc(done, 1)
                    if j == 0 and c == HALF - 1:
                        turn_x(1)

            def layer2(j):
                if j >= 2:
                    pe.wait_ge(y_ready, j - 1)
                for c in range(C):
                    if c < HALF:
                        pe.wait_ge(act_h_ready, HALF * j + c + 1)
                    else:
                        pe.wait_ge(dve_h_ready, (C - HALF) * j + c - HALF + 1)
                    pe.matmul(y_bank[j % 2][:, 0:D], hT[:, j % 2, c], w2_of(j, c), start=c == 0, stop=False)
                pe.matmul(y_bank[j % 2][:, 0:D], ones_bf[0:3, :], b2_of(j), start=False, stop=True).then_inc(y_ps, 1)

            def step_and_next(j):
                if j + 1 < T:
                    layer1(j)
                    if j:
                        turn_x(j + 1)
                        layer2(j - 1)
                elif j + 1 < J:
                    with pe.If(tiles > j + 1):
                        layer1(j)
                        turn_x(j + 1)
                        layer2(j - 1)
                        step_and_next(j + 1)
                    with pe.Else():
                        layer1(j)
                        layer2(j - 1)
                        layer2(j)
                else:
                    layer1(j)
                    layer2(j - 1)
                    layer2(j)

            keep_warm(WARM[3], bank[0])
            pe.wait_ge(b2_ready, 16)
            pe.wait_ge(experts_loaded, 16 * (2 + S))
            pe.wait_ge(table_ready, 1)
            tiles = pe.value_load(table[0:1, T:T + 1], min_val=T, max_val=J)
            keep_warm(WARM[9], bank[0])
            turn_x(0)
            for j in range(T):
                step_and_next(j)


_INS = ['x', 'ctx_1024', 'L0_xattn_Wq', 'L0_xattn_bq', 'L0_xattn_Wk', 'L0_xattn_bk', 'L0_xattn_Wv', 'L0_xattn_bv',
        'L0_ffn_gate_w', 'L0_ffn_gate_b', 'L0_ffn_w1', 'L0_ffn_b1', 'L0_ffn_w2', 'L0_ffn_b2']


def kernel(**inputs):
    import numpy as _np
    import concourse.bacc as _bacc
    from concourse import mybir as _mybir
    from concourse.bass_utils import run_bass_kernel_spmd as _run

    nc = _bacc.Bacc("TRN2", target_bir_lowering=False, num_devices=1)
    arrays, args = {}, []
    for name in _INS:
        a = _np.ascontiguousarray(inputs[name])
        arrays[f"in_{name}"] = a
        args.append(nc.dram_tensor(f"in_{name}", a.shape, _mybir.dt.from_np(a.dtype), kind="ExternalInput").ap())
    shape = inputs['x'].shape
    args.append(nc.dram_tensor("out_0", shape, _mybir.dt.float32, kind="ExternalOutput").ap())
    xattn_moe_kernel(nc, *args)
    r = _run(nc, [arrays], core_ids=[0])
    return r.results[0]["out_0"]
```

```python
from contextlib import ExitStack

import concourse.bass as bass
from concourse import mybir

F32 = mybir.dt.float32
BF16 = mybir.dt.bfloat16
F16 = mybir.dt.float16
U32 = mybir.dt.uint32
I32 = mybir.dt.int32
ALU = mybir.AluOpType
ACT = mybir.ActivationFunctionType
AX_X = mybir.AxisListType.X

P = 128
EPS = 1e-5
LOG_TINY = -87.33654
BIG = 4096.0


def xattn_moe_kernel(nc, x, ctx_in, Wq, bq, Wk, bk, Wv, bv, gate_w, gate_b, w1, b1, w2, b2, out):
    B, SQ, D = x.shape
    SKV = ctx_in.shape[1]
    E, _, H = w1.shape
    N = B * SQ
    I = SQ // P
    T = B * I
    S = E - 1
    J = S + T
    C = H // P
    SCALE = 1.0 / float(D) ** 0.5
    EXT = D + E
    ROW = EXT + 2
    RING = 8
    LOG_I, LOG_T, LOG_SQ = (n.bit_length() - 1 for n in (I, T, SQ))
    assert D == P and H == C * P and SKV <= P and B == 2 and E == 8 and T == S + 1
    assert (I, T, SQ) == (1 << LOG_I, 1 << LOG_T, 1 << LOG_SQ)

    rows_dram = nc.dram_tensor("token_rows", [N, ROW], F32).ap()

    with ExitStack() as ctx:
        def sb(name, shape, dt=F32):
            return ctx.enter_context(nc.sbuf_tensor(name, shape, dt))

        def sem(name):
            return ctx.enter_context(nc.semaphore(name))

        bank = [ctx.enter_context(nc.psum_tensor(f"bank{i}", [P, 512], F32)) for i in range(8)]

        x_sb = sb("x_sb", [P, B, I, EXT])
        ctx_sb = sb("ctx_sb", [SKV, B, D])
        wq_sb, wk_sb, wv_sb = sb("wq_sb", [P, D]), sb("wk_sb", [P, D]), sb("wv_sb", [P, D])
        bq_sb, bk_sb, bv_sb = sb("bq_sb", [P, 1]), sb("bk_sb", [P, 1]), sb("bv_sb", [1, D])
        bv_col = sb("bv_col", [P, 1])
        gw_sb, gb_sb = sb("gw_sb", [P, E]), sb("gb_sb", [P, E])
        w1_sb = sb("w1_sb", [P, S, H])
        w2_sb = sb("w2_sb", [P, S, C, D])
        b1_sb, b1T = sb("b1_sb", [E * C, P]), sb("b1T", [P, E, C])
        w1_more, w2_more = sb("w1_more", [P, T, H]), sb("w2_more", [P, T, C, D])
        b1_more, b2_more = sb("b1_more", [P, T, C]), sb("b2_more", [P, T, D])
        ident = sb("ident", [P, P])
        centre = sb("centre", [P, P])
        before = sb("before", [P, P], BF16)
        ones_bf = sb("ones_bf", [P, P], BF16)
        ones_row = sb("ones_row", [1, P])
        half = sb("half", [P, I])
        lo_iota = sb("lo_iota", [P, P], F16)
        e_iota = sb("e_iota", [P, E])
        j_iota = sb("j_iota", [P, J])
        j_less_e = sb("j_less_e", [1, T, E])
        thr = sb("thr", [P, T])
        skip0 = sb("skip0", [1, T + 1, E], BF16)
        token = sb("token", [P, T])
        minus_e = sb("minus_e", [P, E + 1])
        warm = sb("warm", [1, 1])
        ctxT, wqT = sb("ctxT", [P, B, SKV]), sb("wqT", [P, P])
        kT = sb("kT", [P, B, SKV])
        score_w = sb("score_w", [P, B, SKV + E])
        bq_share = sb("bq_share", [P, 1])
        vT, v_sb = sb("vT", [P, B, SKV]), sb("v_sb", [SKV, B, EXT])
        stats, mv, varp, rstd = sb("stats", [P, T, 6]), sb("mv", [P, T, 2]), sb("varp", [P, T]), sb("rstd", [P, T])
        std = sb("std", [P, T])
        shift, mean_n = sb("shift", [P, T]), sb("mean_n", [P, T])
        xn, xT = sb("xn", [P, B, I, D]), sb("xT", [P, B, I, P])
        p_sb, pn_sb = sb("p_sb", [P, B, I, SKV]), sb("pn_sb", [P, B, I, SKV])
        smax, nsmax, ssum, sinv = (sb(n, [P, B, I]) for n in ("smax", "nsmax", "ssum", "sinv"))
        pT = sb("pT", [SKV, B, I, P])
        rows = sb("rows", [P, B, I, ROW])
        stats2, mv2, varp2, rstd2 = (sb("stats2", [P, T, 6]), sb("mv2", [P, T, 2]), sb("varp2", [P, T]),
                                     sb("rstd2", [P, T]))
        zr = sb("zr", [P, T, E])
        z, zd, ez = sb("z", [P, T, E]), sb("zd", [P, T, E]), sb("ez", [P, T, E])
        top, top_at = sb("top", [P, T, 8]), sb("top_at", [P, T, 8], U32)
        gap, second, pick = sb("gap", [P, T]), sb("second", [P, T]), sb("pick", [P, T])
        first_best, weight, weighted = (sb(n, [P, T]) for n in ("first_best", "weight", "weighted"))
        esum, inv_esum = sb("esum", [P, T]), sb("inv_esum", [P, T])
        r3, f3 = sb("r3", [P, T, E]), sb("f3", [P, T, E])
        chosen = sb("chosen", [P, T + 1, E], BF16)
        ntile, first = sb("ntile", [P, E + 1]), sb("first", [P, E + 1])
        cmp8, cmpj = sb("cmp8", [P, E, T]), sb("cmpj", [1, T, E])
        expert_f = sb("expert_f", [1, T])
        table = sb("table", [1, T + 1], I32)
        rtok, lo, hi = sb("rtok", [P, T], I32), sb("lo", [P, T], I32), sb("hi", [P, T], I32)
        ftok, tile_of = sb("ftok", [P, T]), sb("tile_of", [P, T])
        own_tile, from_own = sb("own_tile", [P, T]), sb("from_own", [P, T])
        moved = sb("moved", [P, T])
        lo_f, away = sb("lo_f", [P, T]), sb("away", [P, T, P], F16)
        hit = sb("hit", [P, T, 2, J], F16)
        lo_hot = sb("lo_hot", [P, T, P], F16)
        src_row, dst_row = sb("src_row", [P, J], U32), sb("dst_row", [P, J], U32)
        emptyv = sb("emptyv", [P, J])
        row_int, part_p, part_b, part_i, part_pb = (sb(n, [P, J], I32) for n in ("row_int", "part_p", "part_b", "part_i", "part_pb"))
        part_ie = sb("part_ie", [P, J])
        b2_wide = sb("b2_wide", [P, S, D])
        neg_mean, own_scale = sb("neg_mean", [P, T]), sb("own_scale", [P, T])
        centred = sb("centred", [P, T, D])
        first_hot = sb("first_hot", [P, T, P])
        gat = sb("gat", [P, J, ROW])
        xs, xsT = sb("xs", [P, 2, D]), sb("xsT", [P, 2, P])
        hT = sb("hT", [P, 2, C, P])
        xb2 = sb("xb2", [P, 2, D])
        y_sb = sb("y_sb", [P, J, D])

        x_loaded = [sem(f"x_loaded{b}") for b in range(B)]
        ctx_loaded, wq_loaded, wk_loaded, wv_loaded = (sem(n) for n in (
            "ctx_loaded", "wq_loaded", "wk_loaded", "wv_loaded"))
        bk_loaded, gate_loaded, experts_loaded, b1_loaded = (sem(n) for n in (
            "bk_loaded", "gate_loaded", "experts_loaded", "b1_loaded"))
        bq_share_ready = sem("bq_share_ready")
        bq_loaded, gw_loaded, bv_col_loaded = sem("bq_loaded"), sem("gw_loaded"), sem("bv_col_loaded")
        b2_loaded = sem("b2_loaded")
        pool_chain, dve_chain = sem("pool_chain"), sem("dve_chain")
        ident_ready, consts_ready, centre_ready, ones_bf_ready, ones_row_ready, warm_ready = (sem(n) for n in (
            "ident_ready", "consts_ready", "centre_ready", "ones_bf_ready", "ones_row_ready", "warm_ready"))
        ctxT_ps, wqT_ps, kT_ps, sw_ps, vT_ps, v_ps, gwc_ps = (sem(n) for n in (
            "ctxT_ps", "wqT_ps", "kT_ps", "sw_ps", "vT_ps", "v_ps", "gwc_ps"))
        ctxT_ready, wqT_ready, kT_ready, gwc_ready, score_w_ready, vT_ready, v_ready = (sem(n) for n in (
            "ctxT_ready", "wqT_ready", "kT_ready", "gwc_ready", "score_w_ready", "vT_ready", "v_ready"))
        var_ready, rstd_ready, shift_ready = sem("var_ready"), sem("rstd_ready"), sem("shift_ready")
        act_xn_ready, dve_xn_ready, xT_ps, xT_ready = sem("act_xn_ready"), sem("dve_xn_ready"), sem("xT_ps"), sem("xT_ready")
        s_ps, max_ready, p_ready, pT_ps, pT_ready = (sem(n) for n in (
            "s_ps", "max_ready", "p_ready", "pT_ps", "pT_ready"))
        pn_ready, x1_ps, stats_ready = sem("pn_ready"), sem("x1_ps"), sem("stats_ready")
        xg_ready, x1_ready, zd_ready, ez_ready = (sem(n) for n in ("xg_ready", "x1_ready", "zd_ready", "ez_ready"))
        pick_ready, weight_ready, esum_ready = sem("pick_ready"), sem("weight_ready"), sem("esum_ready")
        lo_f_ready, away_ready, act_hot_ready = sem("lo_f_ready"), sem("away_ready"), sem("act_hot_ready")
        lo_ready, pool_hot_ready, means_ready = sem("lo_ready"), sem("pool_hot_ready"), sem("means_ready")
        chosen_ready, rank_ps, hot_ready, slot_ps = (sem(n) for n in (
            "chosen_ready", "rank_ps", "hot_ready", "slot_ps"))
        rows_ready, rows_stored = sem("rows_ready"), sem("rows_stored")
        src_ready, dst_ready, table_ready = sem("src_ready"), sem("dst_ready"), sem("table_ready")
        neg_mean_ready, centred_ready, own_scale_ready = sem("neg_mean_ready"), sem("centred_ready"), sem("own_scale_ready")
        act_first_ready, dve_first_ready = sem("act_first_ready"), sem("dve_first_ready")
        gathered = [sem(f"gathered{k}") for k in range(RING)]
        more_loaded = [sem(f"more_loaded{k}") for k in range(T)]
        late_stored = [sem(f"late_stored{j}") for j in range(T, J)]
        xs_ready, xsT_ps, xsT_ready, y_ps, y_ready, y_stored = (sem(n) for n in (
            "xs_ready", "xsT_ps", "xsT_ready", "y_ps", "y_ready", "y_stored"))
        xb2_ready = sem("xb2_ready")
        act_h_ps, act_h_ready, dve_h_ps, dve_h_ready = (sem(n) for n in (
            "act_h_ps", "act_h_ready", "dve_h_ps", "dve_h_ready"))

        x_dram = x.rearrange("b (p i) d -> b p i d", i=I)
        rows_store = rows_dram.rearrange("(p t) c -> p t c", t=T)
        out_dram = out.rearrange("b s d -> (b s) d")

        s_bank = [bank[0], bank[1]]
        pT_bank, xT_bank = [[bank[2], bank[0]], [bank[3], bank[1]]], [[bank[6], bank[7]], [bank[4], bank[5]]]

        def s_tile(b, i, n=SKV + E):
            return s_bank[b][:, i * (SKV + E):i * (SKV + E) + n]

        def x1_tile(b, i):
            return bank[4 + 2 * b + i // 2][:, (i % 2) * EXT:(i % 2 + 1) * EXT]

        def w1_of(j, c):
            return (w1_sb[:, j] if j < S else w1_more[:, j - S])[:, c * P:(c + 1) * P]

        def w2_of(j, c):
            return w2_sb[:, j, c, :] if j < S else w2_more[:, j - S, c, :]

        def b1_of(j, c):
            return b1T[:, j + 1, c:c + 1] if j < S else b1_more[:, j - S, c:c + 1]

        def b2_of(j):
            return b2_wide[:, j, :] if j < S else b2_more[:, j - S, :]

        xsT_bank = [bank[6], bank[0]]
        act_h_bank, dve_h_bank = [bank[4], bank[2]], [bank[5], bank[3]]
        y_bank = [bank[7], bank[1]]
        HALF = C // 2
        ACT_XN = 1
        POOL_HOT, ACT_HOT = 3, 2
        GATHER_ORDER = [1, 2, 3, 0] + list(range(4, RING))
        ACT_FIRST, DVE_FIRST, FIRST_ORDER = (3, 4, 1, 2), (0, 5, 6, 7), (3, 0, 4, 1, 5, 2, 6, 7)
        WARM_START, WARM_CTX, WARM_ROUTER, WARM_RANK, WARM_FIRST = 28, 9, 80, 44, 3

        block = ctx.enter_context(nc.Block())

        @block.sync
        def _(sp):
            sp.dma_start(x_sb[:, 0, :, 0:D], x_dram[0]).then_inc(x_loaded[0], 16)
            sp.dma_start(x_sb[:, 1, :, 0:D], x_dram[1]).then_inc(x_loaded[1], 16)
            sp.dma_start(bk_sb[:, :], bk.rearrange("(d a) -> d a", a=1)).then_inc(bk_loaded, 16)
            sp.dma_start(bq_sb[:, :], bq.rearrange("(d a) -> d a", a=1)).then_inc(bq_loaded, 16)
            sp.dma_start(gw_sb[:, :], gate_w).then_inc(gw_loaded, 16)
            sp.dma_start(bv_col[:, :], bv.rearrange("(d a) -> d a", a=1)).then_inc(bv_col_loaded, 16)
            sp.dma_start(bv_sb[:, :], bv.rearrange("(a d) -> a d", a=1)).then_inc(wv_loaded, 16)
            sp.dma_start(gb_sb[:, :], gate_b.rearrange("(a e) -> a e", a=1).to_broadcast([P, E])).then_inc(gate_loaded, 16)
            sp.dma_start(b1_sb[:, :], b1.rearrange("e (c q) -> (e c) q", q=P)).then_inc(b1_loaded, 16)
            for lo_e, hi_e in ((1, E // 2), (E // 2, E)):
                sp.dma_start(w1_sb[:, lo_e - 1:hi_e - 1], w1[lo_e:hi_e].rearrange("e d h -> d e h")).then_inc(experts_loaded, 16)
                for e in range(lo_e, hi_e):
                    sp.dma_start(w2_sb[:, e - 1], w2[e].rearrange("(c p) d -> p c d", p=P)).then_inc(experts_loaded, 16)
            sp.dma_start(b2_wide[:, :, :], b2[1:].rearrange("e d -> (e d)").rearrange("(a f) -> a f", a=1)
                         .to_broadcast([P, S * D])).then_inc(b2_loaded, 16)
            for b in range(B):
                sp.wait_ge(x1_ready, 2 * (b + 1))
                sp.dma_start(rows_store[:, b * I:(b + 1) * I, 0:EXT], rows[:, b, :, 0:EXT]).then_inc(rows_stored, 16)
            sp.wait_ge(means_ready, B)
            sp.wait_ge(rows_ready, 1)
            sp.dma_start(rows_store[:, :, EXT:], rows[:, :, :, EXT:].rearrange("p b i c -> p (b i) c")).then_inc(rows_stored, 16)
            sp.wait_ge(table_ready, 1)
            tiles = sp.value_load(table[0:1, T:T + 1], min_val=T, max_val=J)

            def fetch_weights(k):
                e = sp.value_load(table[0:1, k:k + 1], min_val=0, max_val=E - 1)
                here = more_loaded[k]
                sp.dma_start(w1_more[:, k, :], w1[bass.ds(e, 1)].rearrange("e d h -> d (e h)")).then_inc(here, 16)
                sp.dma_start(w2_more[:, k], w2[bass.ds(e, 1)].rearrange("e (c p) d -> p (e c) d", p=P)).then_inc(here, 16)
                sp.dma_start(b1_more[:, k, :], b1T[:, bass.ds(e, 1), :].rearrange("p e c -> p (e c)")).then_inc(here, 16)
                sp.dma_start(b2_more[:, k, :], b2[bass.ds(e, 1)].to_broadcast([P, D])).then_inc(here, 16)

            sp.wait_ge(gathered[1], 16)
            fetch_weights(0)
            with ExitStack() as more:
                for j in range(T, J):
                    more.enter_context(sp.If(tiles > j))
                    fetch_weights(j - S)
            sp.wait_ge(y_stored, 16 * T)
            with ExitStack() as more:
                for j in range(T, J):
                    more.enter_context(sp.If(tiles > j))
                    sp.wait_ge(late_stored[j - T], 16)

        @block.gpsimd
        def _(pool):
            made = [0]

            def step(ins):
                made[0] += 1
                ins.then_inc(pool_chain, 1)

            step(pool.memset(ident[:, :], 0.0))
            pool.memset(ones_bf[:, :], 1.0).then_inc(ones_bf_ready, 1)
            pool.wait_ge(pool_chain, 1)
            pool.affine_select(out=ident[:, :], in_=ident[:, :], compare_op=ALU.not_equal, fill=1.0, base=0,
                               pattern=[[-1, P]], channel_multiplier=1).then_inc(ident_ready, 1)
            step(pool.memset(centre[:, :], -1.0 / D))
            pool.wait_ge(pool_chain, made[0])
            pool.affine_select(out=centre[:, :], in_=centre[:, :], compare_op=ALU.not_equal, fill=1.0 - 1.0 / D, base=0,
                               pattern=[[-1, P]], channel_multiplier=1).then_inc(centre_ready, 1)
            pool.memset(ones_row[:, :], 1.0).then_inc(ones_row_ready, 1)
            step(pool.memset(before[:, :], 1.0))
            step(pool.memset(half[:, :], -0.5))
            step(pool.memset(skip0[:, :, 1:], 0.0))
            step(pool.memset(skip0[:, :, 0:1], float(P)))
            pool.wait_ge(pool_chain, made[0])

            def inverse_root(src, dst, b, at):
                pool.wait_ge(var_ready, at)
                t = slice(b * I, (b + 1) * I)
                pool.tensor_tensor(dst[:, t], src[:, t], half[:, :], ALU.pow).then_inc(rstd_ready, 1)

            for b in range(B):
                inverse_root(varp, rstd, b, b + 1)
            pool.affine_select(out=before[:, :], in_=before[:, :], compare_op=ALU.is_gt, fill=0.0, base=0,
                               pattern=[[1, P]], channel_multiplier=-1)
            pool.memset(minus_e[:, :], -1.0)
            pool.memset(ntile[:, 0:1], 0.0)
            pool.memset(chosen[:, T, :], 0.0)
            for tensor, pattern, base, scale in ((lo_iota, [[1, P]], 0, 0), (e_iota, [[1, E]], 0, 0), (j_iota, [[1, J]], 0, 0),
                                                 (j_less_e, [[1, T], [-1, E]], S - 1, 0), (thr, [[P, T]], P, 0),
                                                 (token, [[1, T]], 0, T)):
                at = tensor[:, :, :] if tensor is j_less_e else tensor[:, :]
                last = pool.iota(at, pattern=pattern, base=base, channel_multiplier=scale,
                                 allow_small_or_imprecise_dtypes=True)
            last.then_inc(consts_ready, 1)
            for b in range(B):
                inverse_root(varp2, rstd2, b, B + b + 1)
            pool.wait_ge(weight_ready, 1)
            step(pool.tensor_tensor(weighted[:, :], weight[:, :], rstd2[:, :], ALU.mult))
            pool.wait_ge(pool_chain, made[0])
            pool.wait_ge(esum_ready, 1)
            pool.tensor_tensor(rows[:, :, :, EXT + 1], weighted[:, :].rearrange("p (b i) -> p b i", b=B),
                               inv_esum[:, :].rearrange("p (b i) -> p b i", b=B), ALU.mult).then_inc(rows_ready, 1)
            pool.wait_ge(lo_ready, 1)
            for t in range(T - POOL_HOT, T):
                ins = pool.tensor_scalar(lo_hot[:, t, :], lo_iota[:, :], lo[:, t:t + 1], None, ALU.is_equal)
            ins.then_inc(pool_hot_ready, 1)

            def gather(j):
                pool.indirect_dma_start(gat[:, j, :], None, rows_dram,
                                        bass.IndirectOffsetOnAxis(src_row[:, j:j + 1], 0)).then_inc(gathered[j % RING], 16)

            def scatter(j):
                pool.wait_ge(y_ready, j + 1)
                pool.indirect_dma_start(out_dram, bass.IndirectOffsetOnAxis(dst_row[:, j:j + 1], 0), y_sb[:, j, :], None,
                                        bounds_check=N - 1, oob_is_err=False).then_inc(
                                            y_stored if j < T else late_stored[j - T], 16)

            pool.wait_ge(rows_stored, 16 * (B + 1))
            pool.wait_ge(src_ready, 1)
            for j in GATHER_ORDER:
                gather(j)
            pool.wait_ge(table_ready, 1)
            tiles = pool.value_load(table[0:1, T:T + 1], min_val=T, max_val=J)
            pool.wait_ge(dst_ready, 1)

            def gather_ahead(j):
                pool.wait_ge(gathered[j % RING], 16 * (j // RING))
                gather(j)

            for j in range(J):
                ahead = j + RING
                if ahead < T:
                    gather_ahead(ahead)
                elif ahead < J:
                    with pool.If(tiles > ahead):
                        gather_ahead(ahead)
                if j < T:
                    scatter(j)
                else:
                    with pool.If(tiles > j):
                        scatter(j)

        @block.scalar
        def _(act):
            act.wait_ge(warm_ready, 1)
            act.activation(warm[:, :], warm[:, :], ACT.Exp)
            act.dma_start(ctx_sb[:, :, :], ctx_in.rearrange("b s d -> s b d")).then_inc(ctx_loaded, 16)
            act.dma_start(wk_sb[:, :], Wk).then_inc(wk_loaded, 16)
            act.dma_start(wq_sb[:, :], Wq).then_inc(wq_loaded, 16)
            act.dma_start(wv_sb[:, :], Wv).then_inc(wv_loaded, 16)
            act.wait_ge(ctxT_ps, 1)
            act.copy(ctxT[:, :, :], bank[0][:, 0:B * SKV].rearrange("p (b s) -> p b s", b=B)).then_inc(ctxT_ready, 1)
            act.wait_ge(bq_loaded, 16)
            act.mul(bq_share[:, :], bq_sb[:, :], 1.0 / D).then_inc(bq_share_ready, 1)
            act.wait_ge(kT_ps, 1)
            act.wait_ge(bk_loaded, 16)
            act.activation(kT[:, :, :], bank[2][:, 0:B * SKV].rearrange("p (b s) -> p b s", b=B), ACT.Identity,
                           bias=bk_sb[:, 0:1]).then_inc(kT_ready, 1)
            act.wait_ge(bq_share_ready, 1)
            act.wait_ge(wqT_ps, 1)
            act.activation(wqT[:, :], bank[1][:, 0:P], ACT.Identity, bias=bq_share[:, 0:1]).then_inc(wqT_ready, 1)

            def evict_pairs(b, to, banks, rows_n, done, ready):
                for h in range(I // 2):
                    act.wait_ge(done, 2 * b + h + 1)
                    act.copy(to[:, b, 2 * h:2 * h + 2], banks[b][h][0:rows_n, 0:2 * P]
                             .rearrange("p (i q) -> p i q", i=2)).then_inc(ready, 1)

            def normalize(b):
                act.wait_ge(x_loaded[b], 16)
                act.wait_ge(shift_ready, b + 1)
                for i in range(ACT_XN):
                    t = b * I + i
                    act.activation(xn[:, b, i], x_sb[:, b, i, 0:D], ACT.Identity, bias=shift[:, t:t + 1],
                                   scale=rstd[:, t:t + 1]).then_inc(act_xn_ready, 1)

            normalize(0)
            act.wait_ge(sw_ps, 1)
            act.copy(score_w[:, :, 0:SKV], bank[3][:, 0:B * SKV].rearrange("p (b s) -> p b s", b=B)).then_inc(
                score_w_ready, 1)
            evict_pairs(0, xT, xT_bank, P, xT_ps, xT_ready)
            normalize(1)
            act.wait_ge(vT_ps, 1)
            act.wait_ge(bv_col_loaded, 16)
            act.activation(vT[:, :, :], bank[2][:, 0:B * SKV].rearrange("p (b s) -> p b s", b=B), ACT.Identity,
                           bias=bv_col[:, 0:1]).then_inc(vT_ready, 1)
            evict_pairs(1, xT, xT_bank, P, xT_ps, xT_ready)

            def exp_scores(b):
                act.wait_ge(max_ready, b + 1)
                for i in range(I):
                    act.activation(p_sb[:, b, i], s_tile(b, i, SKV), ACT.Exp, bias=nsmax[:, b, i:i + 1], scale=SCALE,
                                   accum_out=ssum[:, b, i:i + 1]).then_inc(p_ready, 1)

            exp_scores(0)
            exp_scores(1)
            evict_pairs(0, pT, pT_bank, SKV, pT_ps, pT_ready)
            evict_pairs(1, pT, pT_bank, SKV, pT_ps, pT_ready)
            for k in range(2 * B):
                act.wait_ge(stats_ready, k + 1)
                act.copy(rows[:, k // 2, k % 2 * 2:k % 2 * 2 + 2, 0:EXT],
                         bank[4 + k][:, 0:2 * EXT].rearrange("p (i d) -> p i d", i=2)).then_inc(x1_ready, 1)
            act.wait_ge(neg_mean_ready, 1)
            for t in range(T):
                act.wait_ge(x1_ready, t // 2 + 1)
                act.activation(centred[:, t, :], rows[:, t // I, t % I, 0:D], ACT.Identity,
                               bias=neg_mean[:, t:t + 1]).then_inc(centred_ready, 1)
            act.wait_ge(zd_ready, 1)
            act.activation(ez[:, :, :], zd[:, :, :], ACT.Exp).then_inc(ez_ready, 1)
            act.wait_ge(consts_ready, 1)
            act.wait_ge(lo_f_ready, 1)
            mine = range(T - POOL_HOT - ACT_HOT, T - POOL_HOT)
            for t in mine:
                act.activation(away[:, t, :], lo_iota[:, :], ACT.Abs, bias=lo_f[:, t:t + 1], scale=-1.0).then_inc(away_ready, 1)
            for k, t in enumerate(mine):
                act.wait_ge(away_ready, k + 1)
                act.activation(lo_hot[:, t, :], away[:, t, :], ACT.Relu, bias=1.0, scale=-1.0).then_inc(act_hot_ready, 1)

            def copy_xsT(j):
                act.wait_ge(xsT_ps, j + 1)
                act.copy(xsT[:, j % 2], xsT_bank[j % 2][:, 0:P]).then_inc(xsT_ready, 1)

            def relu_half(j):
                if j >= S:
                    act.wait_ge(more_loaded[j - S], 64)
                act.wait_ge(act_h_ps, j + 1)
                for c in range(HALF):
                    act.activation(hT[:, j % 2, c], act_h_bank[j % 2][:, c * P:(c + 1) * P], ACT.Relu,
                                   bias=b1_of(j, c)).then_inc(act_h_ready, 1)

            act.wait_ge(own_scale_ready, 1)
            act.wait_ge(act_hot_ready, ACT_HOT)
            for t in ACT_FIRST:
                if t not in mine:
                    act.wait_ge(hot_ready, 1)
                act.mul(first_hot[:, t, :], lo_hot[:, t, :], own_scale[:, t:t + 1]).then_inc(act_first_ready, 1)
            act.wait_ge(table_ready, 1)
            tiles = act.value_load(table[0:1, T:T + 1], min_val=T, max_val=J)

            def step_and_next(j):
                if j == 0:
                    relu_half(0)
                    copy_xsT(1)
                elif j + 1 < T:
                    copy_xsT(j + 1)
                    relu_half(j)
                elif j + 1 < J:
                    with act.If(tiles > j + 1):
                        copy_xsT(j + 1)
                        relu_half(j)
                        step_and_next(j + 1)
                    with act.Else():
                        relu_half(j)
                else:
                    relu_half(j)

            copy_xsT(0)
            for j in range(T):
                step_and_next(j)

        @block.vector
        def _(dve):
            made = [0]

            def step(ins):
                made[0] += 1
                ins.then_inc(dve_chain, 1)
                return made[0]

            def settled(at=None):
                dve.wait_ge(dve_chain, made[0] if at is None else at)

            def over_e(a, n=E):
                return a.unsqueeze(2).to_broadcast([a.shape[0], a.shape[1], n])

            def over_t(a, n=T):
                return a.unsqueeze(1).to_broadcast([a.shape[0], n, a.shape[1]])

            def variance(src, b, stats, mv, varp):
                for i in range(I):
                    last = step(dve.bn_stats(stats[:, b * I + i, :], src(i)))
                for i in range(I):
                    settled(last - I + 1 + i)
                    step(dve.bn_aggr(mv[:, b * I + i, :], stats[:, b * I + i, :]))
                settled()
                t = slice(b * I, (b + 1) * I)
                dve.tensor_scalar(varp[:, t], mv[:, t, 1], EPS, None, ALU.add).then_inc(var_ready, 1)

            def row_shift(b):
                ts = slice(b * I, (b + 1) * I)
                dve.wait_ge(rstd_ready, b + 1)
                step(dve.tensor_tensor(mean_n[:, ts], mv[:, ts, 0], rstd[:, ts], ALU.mult))
                settled()
                dve.tensor_scalar(shift[:, ts], mean_n[:, ts], -1.0, 1.0, ALU.mult, ALU.add).then_inc(shift_ready, 1)

            def normalize(t):
                dve.tensor_scalar(xn[:, t // I, t % I], x_sb[:, t // I, t % I, 0:D], rstd[:, t:t + 1], shift[:, t:t + 1],
                                  ALU.mult, ALU.add).then_inc(dve_xn_ready, 1)

            dve.memset(warm[:, :], 0.0).then_inc(warm_ready, 1)
            for b in range(B):
                dve.wait_ge(x_loaded[b], 16)
                variance(lambda i: x_sb[:, b, i, 0:D], b, stats, mv, varp)
            row_shift(0)
            dve.wait_ge(shift_ready, 1)
            for t in range(ACT_XN, I):
                normalize(t)
            dve.wait_ge(gwc_ps, 1)
            dve.tensor_copy(score_w[:, :, SKV:], over_t(bank[4][:, 0:E], B)).then_inc(gwc_ready, 1)
            row_shift(1)
            std_at = step(dve.tensor_tensor(std[:, :], varp[:, :], rstd[:, :], ALU.mult))
            dve.wait_ge(shift_ready, 2)
            for t in range(I + ACT_XN, T):
                normalize(t)

            def row_max(b):
                dve.wait_ge(s_ps, b + 1)
                step(dve.tensor_reduce(smax[:, b], s_bank[b][:, 0:I * (SKV + E)].rearrange(
                    "p (i s) -> p i s", i=I)[:, :, 0:SKV], AX_X, ALU.max))
                settled(std_at)
                dve.tensor_tensor(x_sb[:, b, :, D:], s_bank[b][:, 0:I * (SKV + E)].rearrange(
                    "p (i s) -> p i s", i=I)[:, :, SKV:], over_e(std[:, b * I:(b + 1) * I]), ALU.mult).then_inc(xg_ready, 1)
                settled()
                dve.tensor_scalar(nsmax[:, b], smax[:, b], -SCALE, None, ALU.mult).then_inc(max_ready, 1)

            def softmax(b):
                dve.wait_ge(p_ready, I * (b + 1))
                step(dve.reciprocal(sinv[:, b], ssum[:, b]))
                settled()
                dve.tensor_tensor(pn_sb[:, b], p_sb[:, b], over_e(sinv[:, b], SKV), ALU.mult).then_inc(pn_ready, 1)

            row_max(0)
            row_max(1)
            softmax(0)
            dve.wait_ge(v_ps, 1)
            dve.tensor_copy(v_sb[:, :, :], bank[3][0:SKV, 0:B * EXT].rearrange("p (b d) -> p b d", b=B))
            dve.tensor_copy(b1T[:, :, :], bank[3][:, B * EXT:B * EXT + E * C].rearrange("p (e c) -> p e c", c=C)).then_inc(v_ready, 1)
            softmax(1)
            def first_stats(k):
                t = 2 * k
                dve.wait_ge(x1_ps, k + 1)
                dve.bn_stats(stats2[:, t, :], x1_tile(t // I, t % I)[:, 0:D])

            def second_stats(k):
                t = 2 * k + 1
                dve.bn_stats(stats2[:, t, :], x1_tile(t // I, t % I)[:, 0:D]).then_inc(stats_ready, 1)

            def pair_mean(k):
                dve.wait_ge(stats_ready, k + 1)
                for t in (2 * k, 2 * k + 1):
                    at = step(dve.bn_aggr(mv2[:, t, :], stats2[:, t, :]))
                return at

            def batch_variance(b, means_at):
                settled(means_at)
                ts = slice(b * I, (b + 1) * I)
                dve.tensor_scalar(varp2[:, ts], mv2[:, ts, 1], EPS, None, ALU.add).then_inc(var_ready, 1)

            for k in range(2):
                first_stats(k)
                second_stats(k)
                means_at = pair_mean(k)
            first_stats(2)
            batch_variance(0, means_at)
            second_stats(2)
            first_stats(3)
            second_stats(3)
            pair_mean(2)
            batch_variance(1, pair_mean(3))

            dve.wait_ge(gate_loaded, 16)
            dve.wait_ge(consts_ready, 1)
            def normalized_logits(b):
                dve.wait_ge(x1_ready, 2 * (b + 1))
                dve.wait_ge(rstd_ready, B + b + 1)
                ts = slice(b * I, (b + 1) * I)
                return step(dve.tensor_tensor(zr[:, ts, :], rows[:, b, :, D:EXT], over_e(rstd2[:, ts], E), ALU.mult))

            def logits(b, zr_at):
                ts = slice(b * I, (b + 1) * I)
                settled(zr_at)
                return step(dve.tensor_tensor(z[:, ts, :], zr[:, ts, :], over_t(gb_sb[:, :], I), ALU.add))

            def best_of(b, z_at):
                settled(z_at)
                return [step(dve.max(top[:, t, :], z[:, t, :])) for t in range(b * I, (b + 1) * I)]

            def indices(t, top_ready_at):
                settled(top_ready_at)
                return step(dve.max_index(top_at[:, t, :], top[:, t, :], z[:, t, :]))

            def keep_means(b):
                dve.tensor_copy(rows[:, b, :, EXT], mv2[:, b * I:(b + 1) * I, 0]).then_inc(means_ready, 1)

            zr_at = normalized_logits(0)
            dve.tensor_scalar(neg_mean[:, :], mv2[:, :, 0], -1.0, None, ALU.mult).then_inc(neg_mean_ready, 1)
            z_at = logits(0, zr_at)
            keep_means(0)
            best_at = best_of(0, z_at)
            for i in range(I - 2):
                indices(i, best_at[i])
            keep_means(1)
            zr_at = normalized_logits(1)
            indices(I - 2, best_at[I - 2])
            z_at = logits(1, zr_at)
            indices(I - 1, best_at[I - 1])
            best_at = best_of(1, z_at)
            for i in range(I):
                index_at = indices(I + i, best_at[i])
            step(dve.tensor_tensor(gap[:, :], top[:, :, 1], top[:, :, 0], ALU.subtract))
            dve.tensor_tensor(zd[:, :, :], top[:, :, :], over_e(top[:, :, 0], 8), ALU.subtract).then_inc(zd_ready, 1)
            settled()
            step(dve.scalar_tensor_tensor(out=second[:, :], in0=gap[:, :], scalar=LOG_TINY, in1=top_at[:, :, 1],
                                          op0=ALU.is_gt, op1=ALU.mult))
            settled()
            dve.tensor_tensor(pick[:, :], second[:, :], top_at[:, :, 0], ALU.max).then_inc(pick_ready, 1)
            dve.wait_ge(pick_ready, 1)
            dve.tensor_tensor(chosen[:, 0:T, :], over_t(e_iota[:, :]), over_e(pick[:, :]),
                              ALU.is_equal).then_inc(chosen_ready, 1)
            step(dve.tensor_scalar(own_tile[:, :], pick[:, :], -1.0, None, ALU.add))
            first_at = step(dve.tensor_tensor(first_best[:, :], second[:, :], top_at[:, :, 0], ALU.is_le))
            dve.wait_ge(ez_ready, 1)
            esum_at = step(dve.tensor_reduce(esum[:, :], ez[:, :, :], AX_X, ALU.add))
            settled(first_at)
            dve.tensor_tensor(weight[:, :], first_best[:, :], ez[:, :, 1], ALU.max).then_inc(weight_ready, 1)
            settled(esum_at)
            dve.reciprocal(inv_esum[:, :], esum[:, :]).then_inc(esum_ready, 1)
            rank = bank[2][:, 0:(T + 1) * E].rearrange("p (t e) -> p t e", e=E)
            dve.wait_ge(rank_ps, 1)
            step(dve.tensor_tensor(r3[:, :, :], rank[:, 0:T, :], chosen[:, 0:T, :], ALU.mult))
            step(dve.tensor_tensor(cmp8[:, :, :], over_e(rank[:, T, :], T), over_t(thr[:, :], E), ALU.is_gt))
            settled(made[0] - 1)
            with nc.allow_low_precision("ranks are whole numbers below 2**24"):
                step(dve.tensor_reduce(rtok[:, :], r3[:, :, :], AX_X, ALU.add))
            settled(made[0] - 1)
            step(dve.tensor_reduce(ntile[:, 1:], cmp8[:, :, :], AX_X, ALU.add))
            settled(made[0] - 1)
            dve.tensor_single_scalar(lo[:, :], rtok[:, :], P - 1, ALU.bitwise_and).then_inc(lo_ready, 1)
            hi_at = step(dve.tensor_single_scalar(hi[:, :], rtok[:, :], P.bit_length() - 1, ALU.arith_shift_right))
            settled(made[0] - 1)
            first_at = step(dve.tensor_tensor_scan(first[:, :], minus_e[:, :], ntile[:, :], float(E), ALU.add, ALU.add))
            settled(hi_at)
            dve.wait_ge(lo_ready, 1)
            dve.tensor_copy(lo_f[:, :], lo[:, :]).then_inc(lo_f_ready, 1)
            step(dve.tensor_tensor(from_own[:, :], own_tile[:, :], hi[:, :], ALU.add))
            settled(first_at)
            f3_at = step(dve.tensor_tensor(f3[:, :, :], chosen[:, 0:T, :], over_t(first[:, 0:E]), ALU.mult))
            settled(hi_at)
            dve.wait_ge(lo_ready, 1)
            for t in range(T - POOL_HOT - ACT_HOT):
                if t == 1:
                    settled(f3_at)
                    ftok_at = step(dve.tensor_reduce(ftok[:, :], f3[:, :, :], AX_X, ALU.add))
                if t == 2:
                    settled(ftok_at)
                    moved_at = step(dve.scalar_tensor_tensor(out=moved[:, :], in0=hi[:, :], scalar=0.0, in1=ftok[:, :],
                                                             op0=ALU.is_gt, op1=ALU.mult))
                step(dve.tensor_scalar(lo_hot[:, t, :], lo_iota[:, :], lo[:, t:t + 1], None, ALU.is_equal))
            settled(moved_at)
            tile_at = step(dve.tensor_tensor(tile_of[:, :], from_own[:, :], moved[:, :], ALU.add))
            settled(tile_at)
            step(dve.tensor_tensor(hit[:, :, 1, :], over_e(tile_of[:, :], J), over_t(j_iota[:, :]), ALU.is_equal))
            dve.wait_ge(rows_ready, 1)
            dve.scalar_tensor_tensor(out=own_scale[:, :], in0=tile_of[:, :], scalar=0.0,
                                     in1=rows[:, :, :, EXT + 1].rearrange("p b i -> p (b i)"),
                                     op0=ALU.is_equal, op1=ALU.mult).then_inc(own_scale_ready, 1)
            settled()
            dve.tensor_tensor(hit[:, :, 0, :], hit[:, :, 1, :], over_e(token[:, :], J), ALU.mult).then_inc(hot_ready, 1)
            cmpj_at = step(dve.tensor_tensor(cmpj[:, :, :], over_t(first[0:1, 1:]), j_less_e[:, :, :], ALU.is_le))

            def scale_one_hot(t):
                dve.tensor_scalar(first_hot[:, t, :], lo_hot[:, t, :], own_scale[:, t:t + 1], None, ALU.mult).then_inc(
                    dve_first_ready, 1)

            dve.wait_ge(own_scale_ready, 1)
            scale_one_hot(DVE_FIRST[0])
            dve.wait_ge(slot_ps, 1)
            dve.tensor_copy(src_row[:, :], bank[3][:, 0:J]).then_inc(src_ready, 1)
            dve.wait_ge(pool_hot_ready, 1)
            for t in DVE_FIRST[1:]:
                scale_one_hot(t)
            row_at = step(dve.tensor_copy(row_int[:, :], bank[3][:, 0:J]))
            step(dve.tensor_scalar(emptyv[:, :], bank[3][:, J:2 * J], -BIG, BIG, ALU.mult, ALU.add))
            settled(cmpj_at)
            step(dve.tensor_reduce(expert_f[:, :], cmpj[:, :, :], AX_X, ALU.add))
            step(dve.tensor_scalar(table[:, T:T + 1], first[0:1, E:E + 1], float(E), None, ALU.add))
            settled(made[0] - 1)
            dve.tensor_scalar(table[:, 0:T], expert_f[:, :], float(E - 1), None, ALU.min).then_inc(table_ready, 1)
            settled(row_at)
            step(dve.tensor_scalar(part_p[:, :], row_int[:, :], LOG_T, LOG_I, ALU.arith_shift_right, ALU.arith_shift_left))
            step(dve.tensor_scalar(part_b[:, :], row_int[:, :], I, LOG_SQ - LOG_I, ALU.bitwise_and, ALU.arith_shift_left))
            step(dve.tensor_single_scalar(part_i[:, :], row_int[:, :], I - 1, ALU.bitwise_and))
            settled(made[0] - 1)
            step(dve.tensor_tensor(part_pb[:, :], part_p[:, :], part_b[:, :], ALU.add))
            settled(made[0] - 1)
            step(dve.tensor_tensor(part_ie[:, :], part_i[:, :], emptyv[:, :], ALU.add))
            settled()
            dve.tensor_tensor(dst_row[:, :], part_pb[:, :], part_ie[:, :], ALU.add).then_inc(dst_ready, 1)

            def scale_rows(j):
                dve.wait_ge(gathered[j % RING], 16 * (j // RING + 1))
                dve.tensor_scalar(xs[:, j % 2], gat[:, j, 0:D], gat[:, j, EXT:EXT + 1], gat[:, j, EXT + 1:EXT + 2], ALU.subtract,
                                  ALU.mult).then_inc(xs_ready, 1)

            def relu_half(j):
                if j >= S:
                    dve.wait_ge(more_loaded[j - S], 64)
                dve.wait_ge(dve_h_ps, j + 1)
                for c in range(HALF, C):
                    dve.tensor_scalar(hT[:, j % 2, c], dve_h_bank[j % 2][:, (c - HALF) * P:(c - HALF + 1) * P],
                                      b1_of(j, c), 0.0, ALU.add, ALU.max).then_inc(dve_h_ready, 1)

            def add_b2(j):
                if j >= 2:
                    dve.wait_ge(y_ready, j - 1)
                if j == 0:
                    dve.wait_ge(gathered[0], 16)
                dve.tensor_tensor(xb2[:, j % 2], gat[:, j, 0:D], b2_of(j), ALU.add).then_inc(xb2_ready, 1)

            def add_residual(j):
                dve.wait_ge(xb2_ready, j + 1)
                dve.wait_ge(y_ps, j + 1)
                dve.tensor_tensor(y_sb[:, j, :], y_bank[j % 2][:, 0:D], xb2[:, j % 2], ALU.add).then_inc(y_ready, 1)

            def step_and_next(j):
                if j == 0:
                    scale_rows(1)
                    relu_half(0)
                elif j == 1:
                    scale_rows(2)
                    dve.wait_ge(xsT_ps, 2)
                    scale_rows(3)
                    relu_half(1)
                elif j == 2:
                    relu_half(2)
                    add_b2(0)
                    add_b2(1)
                    add_residual(0)
                elif j + 1 < T:
                    scale_rows(j + 1)
                    add_b2(j - 1)
                    add_residual(j - 2)
                    relu_half(j)
                elif j + 1 < J:
                    with dve.If(tiles > j + 1):
                        scale_rows(j + 1)
                        add_b2(j - 1)
                        add_residual(j - 2)
                        relu_half(j)
                        step_and_next(j + 1)
                    with dve.Else():
                        finish(j)
                else:
                    finish(j)

            def finish(j):
                add_b2(j - 1)
                add_residual(j - 2)
                relu_half(j)
                add_b2(j)
                add_residual(j - 1)
                add_residual(j)

            dve.wait_ge(b2_loaded, 16)
            dve.wait_ge(table_ready, 1)
            tiles = dve.value_load(table[0:1, T:T + 1], min_val=T, max_val=J)
            for j in range(T):
                step_and_next(j)

        @block.tensor
        def _(pe):
            def keep_warm(n, to):
                for _ in range(n):
                    pe.matmul(to[:, 0:P], ones_bf[:, :], ones_bf[:, :], start=True, stop=True)

            pe.wait_ge(ones_bf_ready, 1)
            keep_warm(WARM_START, bank[7])
            pe.wait_ge(ident_ready, 1)
            pe.wait_ge(ctx_loaded, 16)
            for b in range(B):
                ins = pe.transpose(bank[0][:, b * SKV:(b + 1) * SKV], ctx_sb[:, b, :], ident[0:SKV, 0:SKV])
            ins.then_inc(ctxT_ps, 1)
            keep_warm(WARM_CTX, bank[7])
            pe.wait_ge(wk_loaded, 16)
            pe.wait_ge(ctxT_ready, 1)
            ctxT_all = ctxT[:, :, :].rearrange("p b s -> p (b s)")
            pe.matmul(bank[2][:, 0:B * SKV], wk_sb[:, :], ctxT_all, start=True, stop=True).then_inc(kT_ps, 1)
            pe.wait_ge(centre_ready, 1)
            pe.wait_ge(wq_loaded, 16)
            pe.matmul(bank[1][:, 0:P], wq_sb[:, :], centre[:, :], start=True, stop=True).then_inc(wqT_ps, 1)
            pe.wait_ge(gw_loaded, 16)
            pe.matmul(bank[4][:, 0:E], centre[:, :], gw_sb[:, :], start=True, stop=True).then_inc(gwc_ps, 1)

            def transpose_x(b):
                for i in range(I):
                    if i < ACT_XN:
                        pe.wait_ge(act_xn_ready, b * ACT_XN + i + 1)
                    else:
                        pe.wait_ge(dve_xn_ready, b * (I - ACT_XN) + i - ACT_XN + 1)
                    ins = pe.transpose(xT_bank[b][i // 2][:, i % 2 * P:(i % 2 + 1) * P], xn[:, b, i], ident[:, :])
                    if i % 2 == 1:
                        ins.then_inc(xT_ps, 1)

            pe.wait_ge(kT_ready, 1)
            pe.wait_ge(wqT_ready, 1)
            pe.matmul(bank[3][:, 0:B * SKV], wqT[:, :], kT[:, :, :].rearrange("p b s -> p (b s)"),
                      start=True, stop=True).then_inc(sw_ps, 1)
            transpose_x(0)

            def score_pair(b, h):
                pe.wait_ge(xT_ready, 2 * b + h + 1)
                for i in (2 * h, 2 * h + 1):
                    ins = pe.matmul(s_tile(b, i), xT[:, b, i], score_w[:, b], start=True, stop=True)
                if h == I // 2 - 1:
                    ins.then_inc(s_ps, 1)

            pe.wait_ge(wv_loaded, 32)
            pe.matmul(bank[2][:, 0:B * SKV], wv_sb[:, :], ctxT_all, start=True, stop=True).then_inc(vT_ps, 1)
            v_bank = bank[3]

            def values(b):
                o = v_bank[0:SKV, b * EXT:b * EXT + D]
                pe.matmul(o, ctxT[:, b, :], wv_sb[:, :], start=True, stop=False)
                pe.matmul(o, ones_row[:, 0:SKV], bv_sb[:, :], start=False, stop=True)

            pe.wait_ge(ones_row_ready, 1)
            pe.wait_ge(gwc_ready, 1)
            pe.wait_ge(score_w_ready, 1)
            values(0)
            score_pair(0, 0)
            transpose_x(1)
            score_pair(0, 1)
            score_pair(1, 0)
            score_pair(1, 1)
            values(1)
            pe.wait_ge(vT_ready, 1)
            for b in range(B):
                pe.matmul(v_bank[0:SKV, b * EXT + D:(b + 1) * EXT], vT[:, b, :], score_w[:, b, SKV:],
                          start=True, stop=True)
            pe.wait_ge(b1_loaded, 16)
            pe.transpose(v_bank[:, B * EXT:B * EXT + E * C], b1_sb[:, :], ident[0:E * C, 0:E * C]).then_inc(v_ps, 1)

            def transpose_p(b):
                pe.wait_ge(pn_ready, b + 1)
                for i in range(I):
                    ins = pe.transpose(pT_bank[b][i // 2][0:SKV, i % 2 * P:(i % 2 + 1) * P], pn_sb[:, b, i], ident[:, :])
                    if i % 2 == 1:
                        ins.then_inc(pT_ps, 1)

            def add_x(b):
                pe.wait_ge(xg_ready, b + 1)
                for i in range(I):
                    pe.matmul(x1_tile(b, i), ident[:, :], x_sb[:, b, i, :], start=i % 2 == 0, stop=False,
                              skip_group_check=True)

            def attend_pair(b, h):
                pe.wait_ge(pT_ready, 2 * b + h + 1)
                for i in (2 * h, 2 * h + 1):
                    ins = pe.matmul(x1_tile(b, i), pT[:, b, i], v_sb[:, b], start=False, stop=True, skip_group_check=True)
                ins.then_inc(x1_ps, 1)

            add_x(0)
            transpose_p(0)
            add_x(1)
            pe.wait_ge(v_ready, 1)
            attend_pair(0, 0)
            transpose_p(1)
            attend_pair(0, 1)
            attend_pair(1, 0)
            attend_pair(1, 1)
            keep_warm(WARM_ROUTER, bank[2])
            pe.wait_ge(consts_ready, 1)
            pe.wait_ge(chosen_ready, 1)
            rank = bank[2][:, 0:(T + 1) * E]
            pe.matmul(rank, ones_bf[0:1, :], skip0[:, :, :].rearrange("a t e -> a (t e)"), start=True, stop=False,
                      skip_group_check=True)
            for t in range(T):
                pe.matmul(rank[:, (t + 1) * E:], ones_bf[:, :],
                          chosen[:, t, :].unsqueeze(1).to_broadcast([P, T - t, E]),
                          start=False, stop=False, skip_group_check=True)
            pe.matmul(rank, before[:, :], chosen[:, :, :].rearrange("p t e -> p (t e)"), start=False, stop=True,
                      skip_group_check=True).then_inc(rank_ps, 1)
            keep_warm(WARM_RANK, bank[0])
            pe.wait_ge(hot_ready, 1)
            pe.wait_ge(pool_hot_ready, 1)
            pe.wait_ge(act_hot_ready, ACT_HOT)
            for t in range(T):
                ins = pe.matmul(bank[3][:, 0:2 * J], lo_hot[:, t, :], hit[:, t].rearrange("p a j -> p (a j)"),
                                start=t == 0, stop=t == T - 1)
            ins.then_inc(slot_ps, 1)

            pe.wait_ge(centred_ready, T)
            for k, t in enumerate(FIRST_ORDER):
                if t in ACT_FIRST:
                    pe.wait_ge(act_first_ready, ACT_FIRST.index(t) + 1)
                else:
                    pe.wait_ge(dve_first_ready, DVE_FIRST.index(t) + 1)
                ins = pe.matmul(xsT_bank[0][:, 0:P], centred[:, t, :], first_hot[:, t, :], start=k == 0, stop=k == T - 1)
            ins.then_inc(xsT_ps, 1)

            def turn_x(j):
                pe.wait_ge(xs_ready, j)
                pe.transpose(xsT_bank[j % 2][:, 0:P], xs[:, j % 2], ident[:, :]).then_inc(xsT_ps, 1)

            def layer1(j):
                if j >= S:
                    pe.wait_ge(more_loaded[j - S], 64)
                pe.wait_ge(xsT_ready, j + 1)
                for c in range(C):
                    to, at, done = ((act_h_bank, c, act_h_ps) if c < HALF else (dve_h_bank, c - HALF, dve_h_ps))
                    ins = pe.matmul(to[j % 2][:, at * P:(at + 1) * P], w1_of(j, c), xsT[:, j % 2], start=True, stop=True)
                    if c in (HALF - 1, C - 1):
                        ins.then_inc(done, 1)

            def layer2(j):
                if j >= 2:
                    pe.wait_ge(y_ready, j - 1)
                for c in range(C):
                    if c < HALF:
                        pe.wait_ge(act_h_ready, HALF * j + c + 1)
                    else:
                        pe.wait_ge(dve_h_ready, (C - HALF) * j + c - HALF + 1)
                    ins = pe.matmul(y_bank[j % 2][:, 0:D], hT[:, j % 2, c], w2_of(j, c), start=c == 0, stop=c == C - 1)
                    if j == 0 and c == HALF - 1:
                        turn_x(1)
                ins.then_inc(y_ps, 1)

            def step_and_next(j):
                if j == 0:
                    layer1(0)
                    keep_warm(WARM_FIRST, bank[0])
                    layer2(0)
                elif j == 1:
                    turn_x(2)
                    layer1(1)
                elif j + 1 < T:
                    layer1(j)
                    turn_x(j + 1)
                    layer2(j - 1)
                elif j + 1 < J:
                    with pe.If(tiles > j + 1):
                        layer1(j)
                        turn_x(j + 1)
                        layer2(j - 1)
                        step_and_next(j + 1)
                    with pe.Else():
                        layer1(j)
                        layer2(j - 1)
                        layer2(j)
                else:
                    layer1(j)
                    layer2(j - 1)
                    layer2(j)

            pe.wait_ge(experts_loaded, 16 * (2 + S))
            pe.wait_ge(table_ready, 1)
            tiles = pe.value_load(table[0:1, T:T + 1], min_val=T, max_val=J)
            for j in range(T):
                step_and_next(j)


_INS = ['x', 'ctx_1024', 'L0_xattn_Wq', 'L0_xattn_bq', 'L0_xattn_Wk', 'L0_xattn_bk', 'L0_xattn_Wv', 'L0_xattn_bv',
        'L0_ffn_gate_w', 'L0_ffn_gate_b', 'L0_ffn_w1', 'L0_ffn_b1', 'L0_ffn_w2', 'L0_ffn_b2']


def kernel(**inputs):
    import numpy as _np
    import concourse.bacc as _bacc
    from concourse import mybir as _mybir
    from concourse.bass_utils import run_bass_kernel_spmd as _run

    nc = _bacc.Bacc("TRN2", target_bir_lowering=False, num_devices=1)
    arrays, args = {}, []
    for name in _INS:
        a = _np.ascontiguousarray(inputs[name])
        arrays[f"in_{name}"] = a
        args.append(nc.dram_tensor(f"in_{name}", a.shape, _mybir.dt.from_np(a.dtype), kind="ExternalInput").ap())
    shape = inputs['x'].shape
    args.append(nc.dram_tensor("out_0", shape, _mybir.dt.float32, kind="ExternalOutput").ap())
    xattn_moe_kernel(nc, *args)
    r = _run(nc, [arrays], core_ids=[0])
    return r.results[0]["out_0"]
```
